# Optimizing a Trainium2 kernel written in Bass

```python
import numpy as np
import jax
import jax.numpy as jnp

def _softmax(x, axis=-1):
    return jax.nn.softmax(x, axis=axis)

def _gelu(x):
    return jax.nn.gelu(x, approximate=True)

def _silu(x):
    return jax.nn.silu(x)

def _sigmoid(x):
    return jax.nn.sigmoid(x)

def _layernorm(x, axis=-1, eps=1e-05):
    m = jnp.mean(x, axis=axis, keepdims=True)
    v = jnp.var(x, axis=axis, keepdims=True)
    return (x - m) / jnp.sqrt(v + eps)

def _scatter_add(tgt, idx, src, axis=0):
    return tgt.at[idx].add(src)

def _segment_sum(src, seg, n):
    return jax.ops.segment_sum(src, seg, n)
kernel_name = 'mk_adj_ffn_d1_adj_r2_5acef4'

def setup_inputs(seed: int=0):
    np.random.seed(seed)
    _w = jnp.asarray

    def _rec_inputs():
        import jax
        import jax.numpy as jnp
        _gk = jax.random.key(seed)
        x = -0.0005207 + 1.001 * jax.random.normal(jax.random.fold_in(_gk, 1), (32, 256, 128), jnp.float32)
        _w = (1.0 + jnp.arange(256, dtype=jnp.float32)) ** (-0.5)
        _w = _w / _w.mean()
        _pij = jnp.clip(0.0625 * _w[:, None] * _w[None, :], 0.0, 1.0)
        _a = jax.random.uniform(jax.random.fold_in(_gk, 2), (32, 256, 256)) < _pij
        _a = jnp.logical_or(_a, jnp.eye(256, dtype=bool))
        _af = _a.astype(jnp.float32)
        _af = _af * jax.random.uniform(jax.random.fold_in(_gk, 3), (32, 256, 256), jnp.float32, 0.05, 1)
        adj = _af
        return (x, adj)
    x, adj = _rec_inputs()

    def _L0_gnn_setup():
        import math
        import jax, jax.numpy as jnp
        import numpy as np
        HIDDEN = 128
        HEADS = 8
        HEAD_DIM = HIDDEN // HEADS
        key = jax.random.key(seed)
        ks = jax.random.split(key, 8)
        b, n = (2, 2048)
        node_state = jax.random.normal(ks[0], (b, n, HIDDEN), dtype=jnp.float32)
        adjacency = jax.random.uniform(ks[1], (b, n, n), dtype=jnp.float32)
        s = 1.0 / math.sqrt(HIDDEN)
        Wq = jax.random.uniform(ks[2], (HIDDEN, HIDDEN), jnp.float32, -s, s)
        Wk = jax.random.uniform(ks[3], (HIDDEN, HIDDEN), jnp.float32, -s, s)
        Wv = jax.random.uniform(ks[4], (HIDDEN, HIDDEN), jnp.float32, -s, s)
        Wo = jax.random.uniform(ks[5], (HIDDEN, HIDDEN), jnp.float32, -s, s)
        bo = jax.random.uniform(ks[6], (HIDDEN,), jnp.float32, -s, s)
        return {'node_state': node_state, 'adjacency': adjacency, 'Wq': Wq, 'Wk': Wk, 'Wv': Wv, 'Wo': Wo, 'bo': bo}
    _L0_gnn_all = _L0_gnn_setup()
    _L0_gnn_in = {k: v for k, v in _L0_gnn_all.items() if k in ('Wq', 'Wk', 'Wv', 'Wo', 'bo')}
    del _L0_gnn_all

    def _L0_ffn_setup():
        import jax, jax.numpy as jnp
        import numpy as np
        B, S, D, H, E, K = (8, 4096, 128, 512, 8, 2)
        key = jax.random.key(seed)
        ks = jax.random.split(key, 7)
        s_in = 1.0 / np.sqrt(D)
        s_hid = 1.0 / np.sqrt(H)
        return {'x': jax.random.normal(ks[0], (B, S, D), dtype=jnp.float32), 'Wg': jax.random.uniform(ks[1], (E, D), jnp.float32, -s_in, s_in), 'bg': jax.random.uniform(ks[2], (E,), jnp.float32, -s_in, s_in), 'W1': jax.random.uniform(ks[3], (E, H, D), jnp.float32, -s_in, s_in), 'b1': jax.random.uniform(ks[4], (E, H), jnp.float32, -s_in, s_in), 'W2': jax.random.uniform(ks[5], (E, D, H), jnp.float32, -s_hid, s_hid), 'b2': jax.random.uniform(ks[6], (E, D), jnp.float32, -s_hid, s_hid)}
    _L0_ffn_all = _L0_ffn_setup()
    _L0_ffn_in = {k: v for k, v in _L0_ffn_all.items() if k in ('Wg', 'bg', 'W1', 'b1', 'W2', 'b2')}
    del _L0_ffn_all
    return {'x': x, 'adj': adj, 'L0_gnn_Wq': _L0_gnn_in['Wq'], 'L0_gnn_Wk': _L0_gnn_in['Wk'], 'L0_gnn_Wv': _L0_gnn_in['Wv'], 'L0_gnn_Wo': _L0_gnn_in['Wo'], 'L0_gnn_bo': _L0_gnn_in['bo'], 'L0_ffn_Wg': _L0_ffn_in['Wg'], 'L0_ffn_bg': _L0_ffn_in['bg'], 'L0_ffn_W1': _L0_ffn_in['W1'], 'L0_ffn_b1': _L0_ffn_in['b1'], 'L0_ffn_W2': _L0_ffn_in['W2'], 'L0_ffn_b2': _L0_ffn_in['b2']}

def reference(x, adj, L0_gnn_Wq, L0_gnn_Wk, L0_gnn_Wv, L0_gnn_Wo, L0_gnn_bo, L0_ffn_Wg, L0_ffn_bg, L0_ffn_W1, L0_ffn_b1, L0_ffn_W2, L0_ffn_b2):
    import jax
    import jax.numpy as jnp

    def _L0_gnn_ref(node_state, adjacency, Wq, Wk, Wv, Wo, bo):
        import math
        import jax, jax.numpy as jnp
        import numpy as np
        HIDDEN = 128
        HEADS = 8
        HEAD_DIM = HIDDEN // HEADS
        b, n, _ = node_state.shape

        def split_heads(x):
            return x.reshape(b, n, HEADS, HEAD_DIM).transpose(0, 2, 1, 3)
        q = split_heads(node_state @ Wq.T)
        k = split_heads(node_state @ Wk.T)
        v = split_heads(node_state @ Wv.T)
        scores = jnp.einsum('bhqd,bhkd->bhqk', q, k) / math.sqrt(HEAD_DIM)
        log_adj = jnp.log(adjacency + 1e-06)
        scores = scores + log_adj[:, None, :, :]
        attn = jax.nn.softmax(scores, axis=-1)
        out = jnp.einsum('bhqk,bhkd->bhqd', attn, v)
        out = out.transpose(0, 2, 1, 3).reshape(b, n, HIDDEN)
        return out @ Wo.T + bo

    def _L0_ffn_ref(x, Wg, bg, W1, b1, W2, b2):
        import jax, jax.numpy as jnp
        import numpy as np
        B, S, D, H, E, K = (8, 4096, 128, 512, 8, 2)
        gate_scores = jnp.einsum('bsd,ed->bse', x, Wg) + bg
        topk_scores, topk_idx = jax.lax.top_k(gate_scores, K)
        topk_probs = jax.nn.softmax(topk_scores, axis=-1)
        combine = jnp.sum(topk_probs[..., None] * jax.nn.one_hot(topk_idx, E, dtype=x.dtype), axis=-2)
        out = jnp.zeros_like(x)
        for e in range(E):
            h = jax.nn.relu(jnp.einsum('bsd,hd->bsh', x, W1[e]) + b1[e])
            y = jnp.einsum('bsh,dh->bsd', h, W2[e]) + b2[e]
            out = out + combine[..., e:e + 1] * y
        return out
    x = x + _L0_gnn_ref(_layernorm(x, axis=-1), adj, L0_gnn_Wq, L0_gnn_Wk, L0_gnn_Wv, L0_gnn_Wo, L0_gnn_bo)
    x = x + _L0_ffn_ref(_layernorm(x, axis=-1), L0_ffn_Wg, L0_ffn_bg, L0_ffn_W1, L0_ffn_b1, L0_ffn_W2, L0_ffn_b2)
    return x

_drawn_inputs = setup_inputs


def setup_inputs(seed=0):
    import zlib

    import numpy as np

    out = dict(_drawn_inputs(seed))
    spreads = {}
    factors = {'L0_ffn_b1': 3.884, 'L0_ffn_b2': 3.085}
    for name, (base, spread) in spreads.items():
        noise = np.random.default_rng([zlib.crc32(name.encode()), seed]).standard_normal(out[name].shape)
        drawn = base * np.exp(spread * noise) if base else spread * noise
        out[name] = jnp.asarray(drawn.astype(out[name].dtype))
    for name, factor in factors.items():
        out[name] = (out[name] * factor).astype(out[name].dtype)
    return out
```

```python
from contextlib import ExitStack

import concourse.bass as bass
from concourse import mybir

P = 128
F32 = mybir.dt.float32
BF16 = mybir.dt.bfloat16
U32 = mybir.dt.uint32
I32 = mybir.dt.int32
ALU = mybir.AluOpType
ACT = mybir.ActivationFunctionType
AX = mybir.AxisListType
ds = bass.ds

HEADS = 8
SLOTS = 2
LN_EPS = 1e-5
ADJ_EPS = 1e-6
PARTS = 3
Q_PARTS = (0, 1, 2, 0, 1, 0)
K_PARTS = (0, 0, 0, 1, 1, 2)
DMA = 16


def wait_apart(eng, waited, sem, value):
    if isinstance(value, int):
        if value > 0:
            eng.wait_ge(sem, value)
        return
    eng.wait_ge(sem, value)
    eng.sem_inc(waited, 1)


class Chain:

    def __init__(self, eng, sem, waited):
        self.eng, self.sem, self.waited = eng, sem, waited
        self.n, self.i, self.per, self.k = 0, None, 0, 0

    def enter(self, i, per):
        self.i, self.per, self.k = i, per, 0

    def leave(self, times):
        assert self.k == self.per, (self.k, self.per)
        self.n += times * self.per
        self.i, self.k = None, 0

    def value(self):
        return self.n + self.k if self.i is None else self.i * self.per + (self.n + self.k)

    def count(self, ins):
        ins.then_inc(self.sem, 1)
        self.k += 1
        if self.i is None:
            self.n, self.k = self.n + 1, 0

    def __call__(self, ins):
        self.count(ins)
        self.eng.wait_ge(self.sem, self.value())

    def apart(self, ins):
        self.count(ins)
        wait_apart(self.eng, self.waited, self.sem, self.value())


class Experts:

    def __init__(self, eng, table):
        self.eng, self.table, self.at, self.word = eng, table, None, None

    def __call__(self, t, i, u, off):
        if isinstance(t, int):
            i, u = (t + off) // 4, (t + off) % 4 - off
        if self.at is not i:
            at = self.table[0:1, i:i + 1] if isinstance(i, int) else self.table[0:1, ds(i, 1)]
            self.at, self.word = i, self.eng.value_load(at, min_val=0, max_val=2 ** 18 - 1)
        return (self.word >> (3 * (u + off + 1))) & 7


def adj_moe_kernel(nc, x, adj, Wq, Wk, Wv, Wo, bo, Wg, bg, W1, b1, W2, b2, out):
    NB, N, D = x.shape
    E, F, _ = W1.shape
    HD = D // HEADS
    NC = N // P
    NT = NB * NC
    T = NT * P
    FC = F // P
    HG = 4
    VW = P // HG
    GR = NC * HEADS // 2
    KS = len(Q_PARTS) * HD
    ROW = D + 2
    CAP = T + P
    NTILES = (SLOTS * T + E * (P - 1)) // P
    NTILES += -NTILES % 4
    SURPLUS = NTILES - SLOTS * T // P
    PADS = E + SURPLUS
    WR = 4
    CG = 4
    assert D == P and N == 2 * P and GR == 8 and NB % 2 == 0 and FC == 4

    xs = nc.dram_tensor("routed_rows", [E * CAP + SURPLUS * P, ROW], F32, kind="Internal").ap()
    ys = nc.dram_tensor("slot_results", [SLOTS * T + PADS * P, D], F32, kind="Internal").ap()
    parts_dram = nc.dram_tensor("qk_parts", [2, P, PARTS, 2 * N], BF16, kind="Internal").ap()

    x_v = x.rearrange("b (c p) d -> b p c d", p=P)
    adj_v = adj.rearrange("b (c p) k -> b p c k", p=P)
    out_v = out.rearrange("b (c p) d -> p (b c) d", p=P)

    with ExitStack() as ctx:
        def sb(name, shape, dt=F32):
            return ctx.enter_context(nc.sbuf_tensor(name, shape, dt))

        def sem(name):
            return ctx.enter_context(nc.semaphore(name))

        psS = ctx.enter_context(nc.psum_tensor("psS", [P, 2, 512], F32))
        psT = ctx.enter_context(nc.psum_tensor("psT", [P, 2, 512], F32))
        psO = ctx.enter_context(nc.psum_tensor("psO", [P, 512], F32))
        psX = ctx.enter_context(nc.psum_tensor("psX", [P, 512], F32))
        psQ = ctx.enter_context(nc.psum_tensor("psQ", [P, 512], F32))
        psR = ctx.enter_context(nc.psum_tensor("psR", [P, 512], F32))

        ident = sb("ident", [P, P])
        before = sb("before", [P, P], BF16)
        ones_bf = sb("ones_bf", [P, P], BF16)
        neg_half = sb("neg_half", [P, 2])
        adj_eps = sb("adj_eps", [P, 1])
        iota_e = sb("iota_e", [P, E])
        w_raw = sb("w_raw", [P, 4, P])
        wT = sb("wT", [P, 4, P])
        wg_raw = sb("wg_raw", [E, D])
        wgT = sb("wgT", [P, E])
        bo_bc = sb("bo_bc", [P, D])
        bg_bc = sb("bg_bc", [P, E])
        b1_bc = sb("b1_bc", [P, E * F])
        b2_bc = sb("b2_bc", [P, E * D])
        w1_raw = sb("w1_raw", [P, WR, FC * D])
        w2_raw = sb("w2_raw", [P, WR, F])
        w1T = sb("w1T", [P, E * F])
        w2T = sb("w2T", [P, E * FC * D])

        xin = sb("xin", [P, 2, NC * D])
        adj_in = sb("adj_in", [P, 2, NC * N])
        x1 = sb("x1", [P, NT * D])
        stats = sb("stats", [P, NC, 6])
        mv = sb("mv", [P, 2, NC, 2])
        rstd = sb("rstd", [P, 2, NC])
        var_e = sb("var_e", [P, NC])
        xn = sb("xn", [P, 2, NC * D])
        xT = sb("xT", [P, 2, N])
        qk = sb("qk", [P, 2 * N])
        rest = sb("rest", [P, 2 * N])
        parts = sb("parts", [P, 2, PARTS, 2 * N], BF16)
        qp = sb("qp", [KS, 2, HEADS, N], BF16)
        kp = sb("kp", [KS, 2, HEADS, N], BF16)
        vaug = sb("vaug", [P, 2, NC, HEADS, VW])
        adjT = sb("adjT", [P, 2, NC, N])
        nmax = sb("nmax", [P, 4, 2])
        ex = sb("ex", [P, 2, 512])
        pT = sb("pT", [P, 2, 512])
        o_sb = sb("o_sb", [P, 512])
        rec = sb("rec", [P, 16])
        on = sb("on", [P, NC * D])
        onT = sb("onT", [P, NC * D])
        stats2 = sb("stats2", [P, NC, 6])
        mv2 = sb("mv2", [P, NC, 2])
        var2 = sb("var2", [P, NC])
        rstd2 = sb("rstd2", [P, NC])
        rows = sb("rows", [P, 2, NC, SLOTS, ROW])
        x2T = sb("x2T", [P, N])
        gate = sb("gate", [P, NC, E])
        top = sb("top", [P, NC, 8])
        topi = sb("topi", [P, NC, 8], U32)
        topf = sb("topf", [P, NC, SLOTS])
        onehot = sb("onehot", [P, NC, SLOTS, E])
        member = sb("member", [P, NC, E], BF16)
        gap = sb("gap", [P, NC])
        egap = sb("egap", [P, NC])
        den2 = sb("den2", [P, NC])
        base = sb("base", [P, E])
        posn = sb("posn", [P, NC, E])
        possel = sb("possel", [P, NC, SLOTS, E])
        posf = sb("posf", [P, NC, SLOTS])
        posi = sb("posi", [P, 2, NC * SLOTS], U32)
        dest = sb("dest", [P, NC, SLOTS])

        part_i = sb("part_i", [P, 1])
        padrow = sb("padrow", [P, PADS, ROW])
        padf = sb("padf", [P, E])
        padi = sb("padi", [P, E], U32)
        ebase = sb("ebase", [P, E])
        cnt_i = sb("cnt_i", [P, E], I32)
        cnt_t = sb("cnt_t", [P, E], I32)
        ntile = sb("ntile", [P, E])
        endt = sb("endt", [P, E])
        iota_t = sb("iota_t", [1, NTILES])
        past = sb("past", [1, NTILES, E])
        pastw = sb("pastw", [1, NTILES, E])
        te = sb("te", [1, NTILES])
        tep = sb("tep", [1, NTILES + 2])
        tw = sb("tw", [1, NTILES])
        ta = sb("ta", [1, NTILES])
        tb = sb("tb", [1, NTILES])
        packf = sb("packf", [1, NTILES // 4])
        tab_e = sb("tab_e", [1, NTILES // 4], I32)
        tab_row = sb("tab_row", [1, NTILES], I32)

        xr = sb("xr", [P, 4, ROW])
        xrT = sb("xrT", [P, 2, P])
        hb = sb("hb", [P, 2, F])
        hT = sb("hT", [P, 2, FC * P])
        yb = sb("yb", [P, 2, D])
        yw = sb("yw", [P, 4, D])
        yi = sb("yi", [P, 4], U32)
        yp = sb("yp", [P, 4])

        yin = w1T[:, 0:2 * CG * SLOTS * D].rearrange("p (u c d) -> p u c d", u=2, c=CG)
        ysum = w2T[:, 0:2 * CG * D].rearrange("p (u c d) -> p u c d", u=2, c=CG)

        s_const = sem("s_const")
        s_waited = sem("s_waited")
        s_pc = sem("s_pc")
        s_w = sem("s_w")
        s_wl = [sem(f"s_wl{r}") for r in range(WR)]
        s_b = sem("s_b")
        s_wt = sem("s_wt")
        s_wts = sem("s_wts")
        s_dc = sem("s_dc")
        s_xin = [sem(f"s_xin{p}") for p in range(2)]
        s_adjin = [sem(f"s_adjin{p}") for p in range(2)]
        s_store = [sem(f"s_store{p}") for p in range(2)]
        s_pack = [sem(f"s_pack{p}") for p in range(2)]
        s_ln = sem("s_ln")
        s_rstd = sem("s_rstd")
        s_xn = sem("s_xn")
        s_xb = sem("s_xb")
        s_xTp = sem("s_xTp")
        s_xT = sem("s_xT")
        s_qkp = sem("s_qkp")
        s_qk = sem("s_qk")
        s_parts = sem("s_parts")
        s_vp = sem("s_vp")
        s_v = sem("s_v")
        s_ap = sem("s_ap")
        s_a = sem("s_a")
        s_s = sem("s_s")
        s_max = sem("s_max")
        s_exp = sem("s_exp")
        s_t = sem("s_t")
        s_mul = sem("s_mul")
        s_av = sem("s_av")
        s_o = sem("s_o")
        s_otp = sem("s_otp")
        s_on = sem("s_on")
        s_ontp = sem("s_ontp")
        s_ont = sem("s_ont")
        s_y = sem("s_y")
        s_ln2 = sem("s_ln2")
        s_rstd2 = sem("s_rstd2")
        s_x2 = sem("s_x2")
        s_x2c = sem("s_x2c")
        s_x2tp = sem("s_x2tp")
        s_x2t = sem("s_x2t")
        s_gate = sem("s_gate")
        s_top = sem("s_top")
        s_gexp = sem("s_gexp")
        s_rank = sem("s_rank")
        s_pos = sem("s_pos")
        s_sc = [sem(f"s_sc{p}") for p in range(2)]
        s_pad = sem("s_pad")
        s_padd = sem("s_padd")
        s_tab = sem("s_tab")
        s_ac = sem("s_ac")
        s_w1 = sem("s_w1")
        s_w2 = sem("s_w2")
        s_wp = sem("s_wp")
        f_in = [sem(f"f_in{p}") for p in range(4)]
        f_meta = sem("f_meta")
        f_xp = sem("f_xp")
        f_xT = sem("f_xT")
        f_h = sem("f_h")
        f_hb = sem("f_hb")
        f_hp = sem("f_hp")
        f_hT = sem("f_hT")
        f_y = sem("f_y")
        f_yw = sem("f_yw")
        f_sc = [sem(f"f_sc{p}") for p in range(4)]
        c_in = [sem(f"c_in{p}") for p in range(2)]
        c_add = sem("c_add")
        c_sum = sem("c_sum")
        c_out = sem("c_out")

        block = ctx.enter_context(nc.Block())

        def ge_apart(eng, s, v):
            wait_apart(eng, s_waited, s, v)

        def group_of(m):
            return m // (GR // NC), 2 * (m % (GR // NC))

        def has(v, off, count):
            return not isinstance(v, int) or 0 <= v + off < count

        def ge(eng, s, v):
            if not isinstance(v, int) or v > 0:
                eng.wait_ge(s, v)

        def pipeline(eng, body, lo, first, times, step, hi, chains=()):
            for v in range(lo, first):
                body(v, v // step, v % step)
            with eng.Fori(0, times) as it:
                for chain, per in chains:
                    chain.enter(it, per)
                i = it + first // step
                for u in range(step):
                    body(it * step + (first + u), i, u)
            for chain, _ in chains:
                chain.leave(times)
            for v in range(first + step * times, hi):
                body(v, v // step, v % step)

        def batches(eng, body, chains=()):
            pipeline(eng, body, -4, 2, (NB - 6) // 2, 2, NB + 2, chains)

        def tiles(eng, body, chains=()):
            pipeline(eng, body, -2, 4, NTILES // 4 - 2, 4, NTILES + 1, chains)

        def use(i, par, off):
            return i + (par + off) // 2, (par + off) % 2

        def batch_of(view, b):
            return view[b] if isinstance(b, int) else view[ds(b, 1)].rearrange("o p c d -> (o p) c d")

        def tile_span(t, n):
            return slice(t * D, (t + n) * D) if isinstance(t, int) else ds(t * D, n * D)

        def chunks(ap):
            return ap.rearrange("p (c d) -> p c d", c=NC)

        @block.sync
        def _(sp):
            for k, w in enumerate((Wq, Wk, Wv, Wo)):
                sp.dma_start(w_raw[:, k, :], w).then_inc(s_w, DMA)
            sp.dma_start(wg_raw[:, :], Wg).then_inc(s_w, DMA)
            sp.dma_start(bo_bc[:, :], bo.unsqueeze(0).broadcast_to([P, D])).then_inc(s_w, DMA)
            sp.dma_start(bg_bc[:, :], bg.unsqueeze(0).broadcast_to([P, E])).then_inc(s_w, DMA)

            def expert_matrices(e):
                sp.dma_start(w1_raw[:, e % WR, :].rearrange("p (c d) -> p c d", c=FC),
                             W1[e].rearrange("(c p) d -> p c d", p=P)).then_inc(s_wl[e % WR], DMA)
                sp.dma_start(w2_raw[:, e % WR, :], W2[e]).then_inc(s_wl[e % WR], DMA)

            def body(b, i, par):
                if has(b, 4, NB):
                    _, q = use(i, par, 4)
                    ge_apart(sp, s_xn, b + 3)
                    ge(sp, s_xb, b + 3)
                    sp.dma_start(chunks(xin[:, q, :]), batch_of(x_v, b + 4)).then_inc(s_xin[q], DMA)
                if has(b, 2, NB):
                    h, q = use(i, par, 2)
                    ge_apart(sp, s_ap, b + 1)
                    sp.dma_start(chunks(adj_in[:, q, :]), batch_of(adj_v, b + 2)).then_inc(s_adjin[q], DMA)
                    ge_apart(sp, s_parts, b + 3)
                    ge(sp, s_pack[q], DMA * 2 * len(Q_PARTS) * h)
                    sp.dma_start(parts_dram[q], parts[:, q, :, :]).then_inc(s_store[q], DMA)
                    ge_apart(sp, s_store[q], DMA * (h + 1))
                    ge_apart(sp, s_s, GR * (b + 1))
                    src = parts_dram[q].rearrange("(h d) s t -> s d h t", h=HEADS)
                    for k in range(len(Q_PARTS)):
                        rows_k = slice(HD * k, HD * (k + 1))
                        sp.dma_start(qp[rows_k, q], src[Q_PARTS[k], :, :, 0:N]).then_inc(s_pack[q], DMA)
                        sp.dma_start(kp[rows_k, q], src[K_PARTS[k], :, :, N:2 * N]).then_inc(s_pack[q], DMA)
                if isinstance(b, int) and b == 1:
                    for e in range(WR):
                        expert_matrices(e)
                    sp.dma_start(b1_bc[:, :], b1.rearrange("e f -> (e f)").unsqueeze(0)
                                 .broadcast_to([P, E * F])).then_inc(s_b, DMA)
                    sp.dma_start(b2_bc[:, :], b2.rearrange("e f -> (e f)").unsqueeze(0)
                                 .broadcast_to([P, E * D])).then_inc(s_b, DMA)

            batches(sp, body)
            for e in range(WR, E):
                sp.wait_ge(s_wp, 2 * (e - WR + 1))
                expert_matrices(e)

            sp.wait_ge(s_tab, 1)
            sp.wait_ge(s_padd, DMA * (E + 1))
            for p in range(2):
                sp.wait_ge(s_sc[p], DMA * NC * SLOTS * (NB // 2))

            def body(t, i, u):
                if has(t, 0, NTILES):
                    first_row = sp.value_load(tab_row[0:1, t:t + 1] if isinstance(t, int) else tab_row[0:1, ds(t, 1)],
                                              min_val=0, max_val=E * CAP + (SURPLUS - 1) * P)
                    ge(sp, f_xp, t - 3)
                    ge_apart(sp, f_meta, t - 3)
                    sp.dma_start(xr[:, u, :], xs[ds(first_row, P)]).then_inc(f_in[u], DMA)

            tiles(sp, body)

            for p in range(4):
                sp.wait_ge(f_sc[p], DMA * (NTILES // 4))
            ys_v = ys[0:SLOTS * T].rearrange("(g c p s) d -> g p c (s d)", c=CG, p=P, s=SLOTS)

            def body(g, i, u):
                ge_apart(sp, c_sum, g - 1)
                sp.dma_start(yin[:, u], ys_v[g] if isinstance(g, int) else
                             ys_v[ds(g, 1)].rearrange("o p c d -> (o p) c d")).then_inc(c_in[u], DMA)

            pipeline(sp, body, 0, 2, NT // CG // 2 - 1, 2, NT // CG)

        @block.gpsimd
        def _(pool):
            g = nc.gpsimd
            link = Chain(pool, s_pc, s_waited)
            link(g.memset(ident[:, :], 1.0))
            link(g.affine_select(out=ident[:, :], in_=ident[:, :], compare_op=ALU.is_equal, fill=0.0,
                                 base=0, pattern=[[-1, P]], channel_multiplier=1))
            link(g.memset(before[:, :], 1.0))
            link(g.affine_select(out=before[:, :], in_=before[:, :], compare_op=ALU.is_gt, fill=0.0,
                                 base=0, pattern=[[1, P]], channel_multiplier=-1))
            link(g.memset(ones_bf[:, :], 1.0))
            link(g.memset(neg_half[:, :], -0.5))
            link(g.memset(adj_eps[:, :], ADJ_EPS))
            link(g.memset(vaug[:, :, :, :, :], 1.0))
            link(g.memset(padrow[:, :, :], 0.0))
            link(g.iota(padrow[:, :, D:D + 1].rearrange("p e o -> p (e o)"), pattern=[[P, PADS]], base=SLOTS * T,
                        channel_multiplier=1, allow_small_or_imprecise_dtypes=True))
            for tile, pattern, mult in ((iota_e[:, :], [[1, E]], 0), (base[:, :], [[CAP, E]], 0),
                                        (ebase[:, :], [[CAP, E]], 0), (part_i[:, :], [[1, 1]], 1),
                                        (iota_t[:, :], [[1, NTILES]], 0),
                                        (dest[:, :, :], [[SLOTS * P, NC], [1, SLOTS]], SLOTS)):
                link(g.iota(tile, pattern=pattern, base=0, channel_multiplier=mult,
                            allow_small_or_imprecise_dtypes=True))
            pool.dma_start(xs[E * CAP:E * CAP + SURPLUS * P].rearrange("(k p) r -> p k r", p=P),
                           padrow[:, E:PADS, :]).then_inc(s_padd, DMA)
            pool.sem_inc(s_const, 1)
            pool.wait_ge(s_w, DMA * 7)

            def body(b, i, par):
                if has(b, 3, NB):
                    h, q = use(i, par, 3)
                    ge_apart(pool, s_ln, b + 4)
                    link(g.tensor_scalar(var_e[:, :], mv[:, q, :, 1], LN_EPS, None, ALU.add))
                    g.tensor_tensor(rstd[:, q, :], var_e[:, :], neg_half[:, :], ALU.pow).then_inc(s_rstd, 1)
                    pool.wait_ge(s_xin[q], DMA * (h + 1))
                    g.tensor_tensor(chunks(x1[:, tile_span((b + 3) * NC, NC)]), chunks(xin[:, q, :]),
                                    bo_bc[:, :].unsqueeze(1).broadcast_to([P, NC, D]), ALU.add).then_inc(s_xb, 1)
                if has(b, 2, NB):
                    h, q = use(i, par, 2)
                    pool.wait_ge(s_qk, b + 3)
                    link.count(g.tensor_tensor(rest[:, :], qk[:, :], parts[:, q, 0, :], ALU.subtract))
                    link(g.tensor_tensor(parts[:, q, 1, :], qk[:, :], parts[:, q, 0, :], ALU.subtract))
                    g.tensor_tensor(parts[:, q, 2, :], rest[:, :], parts[:, q, 1, :],
                                    ALU.subtract).then_inc(s_parts, 1)
                if has(b, -1, NB):
                    ge_apart(pool, s_ln2, b)
                    link(g.tensor_scalar(var2[:, :], mv2[:, :, 1], LN_EPS, None, ALU.add))
                    g.tensor_tensor(rstd2[:, :], var2[:, :], neg_half[:, :], ALU.pow).then_inc(s_rstd2, 1)
                if has(b, -2, NB):
                    _, q = use(i, par, -2)
                    ge_apart(pool, s_pos, b - 1)
                    for c in range(NC):
                        for s in range(SLOTS):
                            k = c * SLOTS + s
                            g.indirect_dma_start(xs, bass.IndirectOffsetOnAxis(ap=posi[:, q, k:k + 1], axis=0),
                                                 rows[:, q, c, s, :], None).then_inc(s_sc[q], DMA)

            batches(pool, body, [(link, 8)])
            pool.wait_ge(s_pad, 1)
            for e in range(E):
                g.indirect_dma_start(xs, bass.IndirectOffsetOnAxis(ap=padi[:, e:e + 1], axis=0),
                                     padrow[:, e, :], None).then_inc(s_padd, DMA)

            def body(t, i, u):
                if has(t, -1, NTILES):
                    v = (u - 1) % 4
                    ge_apart(pool, f_yw, t)
                    g.indirect_dma_start(ys, bass.IndirectOffsetOnAxis(ap=yi[:, v:v + 1], axis=0),
                                         yw[:, v, :], None).then_inc(f_sc[v], DMA)

            tiles(pool, body)

        @block.scalar
        def _(act):
            s = nc.scalar
            act.wait_ge(s_const, 1)

            def exps(b, m, G):
                act.wait_ge(s_max, G + 1)
                ge(act, s_t, G - 1)
                for j in range(2):
                    ins = s.activation(ex[:, m % 2, j * N:(j + 1) * N], psS[:, m % 2, j * N:(j + 1) * N],
                                       ACT.Exp, bias=nmax[:, m % 4, j:j + 1])
                ins.then_inc(s_exp, 1)

            def body(b, i, par):
                for m in range(GR):
                    if m + 2 < GR and has(b, 0, NB) or m + 2 >= GR and has(b, 1, NB):
                        exps(b, (m + 2) % GR, b * GR + (m + 2))
                    if m == 0 and has(b, -1, NB):
                        act.wait_ge(s_av, GR * b)
                        s.activation(o_sb[:, :], psO[:, :], ACT.Copy).then_inc(s_o, 1)
                    if m == 0 and has(b, 2, NB):
                        _, q = use(i, par, 2)
                        act.wait_ge(s_xTp, b + 3)
                        s.activation(xT[:, q, :], psX[:, 0:N], ACT.Copy).then_inc(s_xT, 1)
                    if m == 0 and has(b, -2, NB):
                        act.wait_ge(s_top, b - 1)
                        s.activation(egap[:, :], gap[:, :], ACT.Exp).then_inc(s_gexp, 1)
                    if m == 1 and has(b, 2, NB):
                        h, q = use(i, par, 2)
                        act.wait_ge(s_qkp, b + 3)
                        ge(act, s_parts, b + 2)
                        s.activation(qk[:, :], psQ[:, :], ACT.Copy).then_inc(s_ac, 1)
                        ge(act, s_store[q], DMA * h)
                        s.activation(parts[:, q, 0, :], psQ[:, :], ACT.Copy).then_inc(s_qk, 1)
                    if m == 3 and has(b, 1, NB):
                        _, q = use(i, par, 1)
                        act.wait_ge(s_vp, b + 2)
                        ge(act, s_av, GR * b)
                        s.activation(vaug[:, q, :, :, 0:HD],
                                     psX[:, N:2 * N].rearrange("p (c h d) -> p c h d", c=NC, h=HEADS),
                                     ACT.Copy).then_inc(s_v, 1)
                    if m == 3 and has(b, -1, NB):
                        act.wait_ge(s_ontp, b)
                        s.activation(onT[:, :], psR[:, 0:N], ACT.Copy).then_inc(s_ont, 1)
                    if m == 4 and has(b, 1, NB):
                        _, q = use(i, par, 1)
                        act.wait_ge(s_ap, b + 2)
                        ge(act, s_mul, GR * b)
                        s.activation(adjT[:, q, :, :], psQ[:, :].rearrange("p (c k) -> p c k", c=NC),
                                     ACT.Identity, bias=adj_eps[:, 0:1]).then_inc(s_a, 1)
                    if m == 6 and has(b, -1, NB):
                        _, q = use(i, par, -1)
                        act.wait_ge(s_x2tp, b)
                        s.activation(x2T[:, :], psR[:, 0:N], ACT.Copy).then_inc(s_x2t, 1)
                        s.activation(rows[:, q, :, 1, 0:D], rows[:, q, :, 0, 0:D], ACT.Copy).then_inc(s_x2c, 1)

            batches(act, body)

            for e in range(E):
                act.wait_ge(s_wp, 2 * e + 2)
                s.activation(w2T[:, e * FC * D:(e + 1) * FC * D], psT[:, e % 2, :], ACT.Copy).then_inc(s_w2, 1)

            def body(t, i, u):
                if has(t, 2, NTILES):
                    act.wait_ge(f_xp, t + 3)
                    ge(act, f_h, t + 1)
                    s.activation(xrT[:, u % 2, :], (psX, psO)[u % 2][:, 0:P], ACT.Copy).then_inc(f_xT, 1)
                if has(t, 0, NTILES):
                    act.wait_ge(f_hp, t + 1)
                    ge(act, f_y, t - 1)
                    s.activation(hT[:, u % 2, :], psT[:, u % 2, :], ACT.Relu).then_inc(f_hT, 1)

            tiles(act, body)

            def body(g, i, u):
                act.wait_ge(c_sum, g + 1)
                src = x1[:, tile_span(g * CG, CG)].rearrange("p (c d) -> p c d", c=CG)
                dst = out_v[:, g * CG:(g + 1) * CG, :] if isinstance(g, int) else out_v[:, ds(g * CG, CG), :]
                act.dma_start(dst, src).then_inc(c_out, DMA)

            pipeline(act, body, 0, 2, NT // CG // 2 - 1, 2, NT // CG)
            act.wait_ge(c_out, DMA * (NT // CG))

        @block.vector
        def _(dve):
            v = nc.vector
            link = Chain(dve, s_dc, s_waited)
            dve.wait_ge(s_wt, 1)
            v.tensor_scalar(wT[:, 0, :], psS[:, 0, 0:P], float(HD) ** -0.5, None, ALU.mult).then_inc(s_wts, 1)
            v.tensor_copy(wT[:, 1:4, :].rearrange("p k o -> p (k o)"), psS[:, 0, P:4 * P]).then_inc(s_wts, 1)
            v.tensor_copy(wgT[:, :], psX[:, 0:E]).then_inc(s_wts, 1)
            dve.wait_ge(s_const, 1)
            dve.wait_ge(s_w, DMA * 7)

            def first_norm_stats(b, i, par):
                h, q = use(i, par, 3)
                ge_apart(dve, s_xin[q], DMA * (h + 1))
                for c in range(NC):
                    link.apart(v.bn_stats(stats[:, c, :], xin[:, q, c * D:(c + 1) * D]))
                for c in range(NC):
                    ins = v.bn_aggr(mv[:, q, c, :], stats[:, c, :])
                    if c < NC - 1:
                        link.apart(ins)
                ins.then_inc(s_ln, 1)

            def first_norm(b, i, par):
                _, q = use(i, par, 3)
                dve.wait_ge(s_rstd, b + 4)
                ge(dve, s_xTp, b + 2)
                for c in range(NC):
                    ins = v.tensor_scalar(xn[:, q, c * D:(c + 1) * D], xin[:, q, c * D:(c + 1) * D],
                                          mv[:, q, c, 0:1], rstd[:, q, c:c + 1], ALU.subtract, ALU.mult)
                ins.then_inc(s_xn, 1)

            def normalise(b):
                dve.wait_ge(s_otp, b)
                o = psR[:, :].rearrange("p (k w) -> p k w", w=VW)
                link(v.reciprocal(rec[:, :].unsqueeze(2), o[:, :, HD:HD + 1]))
                v.tensor_tensor(on[:, :].rearrange("p (k d) -> p k d", d=HD), o[:, :, 0:HD],
                                rec[:, :].unsqueeze(2).broadcast_to([P, 16, HD]), ALU.mult).then_inc(s_on, 1)

            def second_norm_stats(b):
                dve.wait_ge(s_y, b)
                dve.wait_ge(s_xb, b)
                r = x1[:, tile_span((b - 1) * NC, NC)]
                link.apart(v.tensor_tensor(r, psR[:, N:2 * N], r, ALU.add))
                for c in range(NC):
                    link.apart(v.bn_stats(stats2[:, c, :], x1[:, tile_span((b - 1) * NC + c, 1)]))
                for c in range(NC):
                    ins = v.bn_aggr(mv2[:, c, :], stats2[:, c, :])
                    if c < NC - 1:
                        link.apart(ins)
                ins.then_inc(s_ln2, 1)

            def second_norm(b, i, par):
                h, q = use(i, par, -1)
                dve.wait_ge(s_rstd2, b)
                ge(dve, s_sc[q], DMA * NC * SLOTS * h)
                for c in range(NC):
                    ins = v.tensor_scalar(rows[:, q, c, 0, 0:D], x1[:, tile_span((b - 1) * NC + c, 1)],
                                          mv2[:, c, 0:1], rstd2[:, c:c + 1], ALU.subtract, ALU.mult)
                ins.then_inc(s_x2, 1)

            def top_two(b):
                dve.wait_ge(s_gate, b)
                link.apart(v.tensor_tensor(gate[:, :, :], psR[:, N:N + NC * E].rearrange("p (c e) -> p c e", c=NC),
                                     bg_bc[:, :].unsqueeze(1).broadcast_to([P, NC, E]), ALU.add))
                for c in range(NC):
                    link.apart(v.max(top[:, c, :], gate[:, c, :]))
                for c in range(NC):
                    link.apart(v.max_index(topi[:, c, :], top[:, c, :], gate[:, c, :]))
                link(v.tensor_copy(topf[:, :, :], topi[:, :, 0:SLOTS]))
                link(v.tensor_tensor(onehot[:, :, :, :],
                                     iota_e[:, :].unsqueeze(1).unsqueeze(1).broadcast_to([P, NC, SLOTS, E]),
                                     topf[:, :, :].unsqueeze(3).broadcast_to([P, NC, SLOTS, E]), ALU.is_equal))
                link(v.tensor_tensor(gap[:, :], top[:, :, 1], top[:, :, 0], ALU.subtract))
                v.tensor_tensor(member[:, :, :], onehot[:, :, 0, :], onehot[:, :, 1, :],
                                ALU.add).then_inc(s_top, 1)

            def places(b, i, par):
                _, q = use(i, par, -2)
                dve.wait_ge(s_gexp, b - 1)
                link(v.tensor_scalar(den2[:, :], egap[:, :], 1.0, None, ALU.add))
                link(v.reciprocal(rows[:, q, :, 0, D + 1:D + 2], den2[:, :].unsqueeze(2)))
                link(v.tensor_tensor(rows[:, q, :, 1, D + 1:D + 2], rows[:, q, :, 0, D + 1:D + 2],
                                     egap[:, :].unsqueeze(2), ALU.mult))
                link(v.tensor_copy(rows[:, q, :, :, D:D + 1], dest[:, :, :].unsqueeze(3)))
                link(v.tensor_scalar(dest[:, :, :], dest[:, :, :], float(SLOTS * N), None, ALU.add))
                dve.wait_ge(s_rank, b - 1)
                o = N + 32
                link(v.tensor_tensor(posn[:, :, :], psR[:, o:o + NC * E].rearrange("p (c e) -> p c e", c=NC),
                                     base[:, :].unsqueeze(1).broadcast_to([P, NC, E]), ALU.add))
                link(v.tensor_tensor(base[:, :], psR[:, o + NC * E:o + NC * E + E], base[:, :], ALU.add))
                link(v.tensor_tensor(possel[:, :, :, :], onehot[:, :, :, :],
                                     posn[:, :, :].unsqueeze(2).broadcast_to([P, NC, SLOTS, E]), ALU.mult))
                link(v.tensor_reduce(posf[:, :, :], possel[:, :, :, :], AX.X, ALU.add))
                dve.wait_ge(s_x2c, b - 1)
                v.tensor_copy(posi[:, q, :], posf[:, :, :].rearrange("p c s -> p (c s)")).then_inc(s_pos, 1)

            def body(b, i, par):
                for m in range(GR):
                    if m + 2 < GR and has(b, 0, NB) or m + 2 >= GR and has(b, 1, NB):
                        m2 = (m + 2) % GR
                        dve.wait_ge(s_s, b * GR + (m + 3))
                        v.tensor_reduce(nmax[:, m2 % 4, :], psS[:, m % 2, :].rearrange("p (j k) -> p j k", j=2),
                                        AX.X, ALU.max, negate=True).then_inc(s_max, 1)
                    if has(b, 0, NB):
                        qc, _ = m // 4, 0
                        G = b * GR + m
                        if m == 0:
                            dve.wait_ge(s_a, b + 1)
                        dve.wait_ge(s_t, G + 1)
                        ge(dve, s_av, G - 1)
                        v.tensor_tensor(pT[:, m % 2, :].rearrange("p (j c q) -> p j c q", j=2, c=NC),
                                        psT[:, m % 2, :].rearrange("p (j c q) -> p j c q", j=2, c=NC),
                                        adjT[:, par, :, qc * P:(qc + 1) * P].unsqueeze(1)
                                        .broadcast_to([P, 2, NC, P]), ALU.mult).then_inc(s_mul, 1)
                    if m == 0 and has(b, 3, NB):
                        first_norm_stats(b, i, par)
                    if m == 1 and has(b, -2, NB):
                        places(b, i, par)
                    if m == 2 and has(b, -1, NB):
                        normalise(b)
                    if m == 2 and has(b, 3, NB):
                        first_norm(b, i, par)
                    if m == 4 and has(b, -1, NB):
                        second_norm_stats(b)
                    if m == 5 and has(b, -1, NB):
                        second_norm(b, i, par)
                    if m == 7 and has(b, -1, NB):
                        top_two(b)

            batches(dve, body, [(link, 2 * 25)])

            link(v.tensor_scalar(padf[:, :], base[:, :], part_i[:, 0:1], None, ALU.add))
            v.tensor_copy(padi[:, :], padf[:, :]).then_inc(s_pad, 1)
            link(v.tensor_tensor(ntile[:, :], base[:, :], ebase[:, :], ALU.subtract))
            link(v.tensor_scalar(cnt_i[:, :], ntile[:, :], float(P - 1), None, ALU.add))
            link(v.tensor_scalar(cnt_t[:, :], cnt_i[:, :], 7, None, ALU.arith_shift_right))
            link(v.tensor_copy(ntile[:, :], cnt_t[:, :]))
            link(v.tensor_copy(endt[:, :], ntile[:, :]))
            for e in range(1, E):
                link(v.tensor_tensor(endt[:, e:e + 1], endt[:, e:e + 1], endt[:, e - 1:e], ALU.add))
            link(v.tensor_tensor(past[:, :, :], iota_t[:, :].unsqueeze(2).broadcast_to([1, NTILES, E]),
                                 endt[0:1, :].unsqueeze(1).broadcast_to([1, NTILES, E]), ALU.is_ge))
            link(v.tensor_reduce(te[:, :], past[:, :, :], AX.X, ALU.add))
            link(v.tensor_tensor(pastw[:, :, :], past[:, :, :],
                                 ntile[0:1, :].unsqueeze(1).broadcast_to([1, NTILES, E]), ALU.mult))
            link(v.tensor_reduce(tw[:, :], pastw[:, :, :], AX.X, ALU.add))
            link(v.tensor_tensor(ta[:, :], iota_t[:, :], tw[:, :], ALU.subtract))
            link(v.memset(tep[:, :], 0.0))
            link(v.tensor_scalar(tep[:, 1:NTILES + 1], te[:, :], float(E - 1), None, ALU.min))
            link(v.memset(packf[:, :], 0.0))
            for k in range(6):
                link(v.scalar_tensor_tensor(out=packf[:, :], in0=tep[:, k:k + NTILES - 3:4], scalar=float(E ** k),
                                            in1=packf[:, :], op0=ALU.mult, op1=ALU.add))
            link(v.tensor_copy(tab_e[:, :], packf[:, :]))
            link(v.tensor_scalar(tb[:, :], te[:, :], float(CAP), None, ALU.mult))
            v.scalar_tensor_tensor(out=tab_row[:, :], in0=ta[:, :], scalar=float(P), in1=tb[:, :],
                                   op0=ALU.mult, op1=ALU.add).then_inc(s_tab, 1)

            for e in range(E):
                dve.wait_ge(s_wp, 2 * e + 1)
                v.tensor_copy(w1T[:, e * F:(e + 1) * F], psS[:, e % 2, :]).then_inc(s_w1, 1)
            dve.wait_ge(s_b, DMA * 2)
            dve.wait_ge(s_tab, 1)

            expert = Experts(dve, tab_e)

            def body(t, i, u):
                if has(t, 1, NTILES):
                    w = (u + 1) % 2
                    e = expert(t, i, u, 1)
                    dve.wait_ge(f_h, t + 2)
                    ge(dve, f_hp, t)
                    v.tensor_tensor(hb[:, w, :], psS[:, w, :], b1_bc[:, ds(e * F, F)], ALU.add).then_inc(f_hb, 1)
                if has(t, 0, NTILES):
                    dve.wait_ge(f_in[u], DMA * (i + 1))
                    ge(dve, f_sc[u], DMA * i)
                    link.count(v.tensor_copy(yi[:, u:u + 1], xr[:, u, D:D + 1]))
                    v.tensor_copy(yp[:, u:u + 1], xr[:, u, D + 1:D + 2]).then_inc(f_meta, 1)
                if has(t, -1, NTILES):
                    w, r = (u - 1) % 2, (u - 1) % 4
                    e = expert(t, i, u, -1)
                    dve.wait_ge(f_y, t)
                    ps = psQ if w == 0 else psR
                    link(v.tensor_tensor(yb[:, w, :], ps[:, 0:D], b2_bc[:, ds(e * D, D)], ALU.add))
                    v.tensor_scalar(yw[:, r, :], yb[:, w, :], yp[:, r:r + 1], None,
                                    ALU.mult).then_inc(f_yw, 1)

            tiles(dve, body, [(link, 8)])

            def body(g, i, u):
                dve.wait_ge(c_in[u], DMA * (i + 1))
                link(v.tensor_tensor(ysum[:, u], yin[:, u, :, 0:D], yin[:, u, :, D:2 * D], ALU.add))
                r = x1[:, tile_span(g * CG, CG)]
                v.tensor_tensor(r, ysum[:, u].rearrange("p c d -> p (c d)"), r, ALU.add).then_inc(c_sum, 1)

            pipeline(dve, body, 0, 2, NT // CG // 2 - 1, 2, NT // CG, [(link, 2)])

        @block.tensor
        def _(pe):
            t_ = nc.tensor
            pe.wait_ge(s_w, DMA * 7)
            pe.wait_ge(s_const, 1)
            for k in range(4):
                t_.transpose(psS[:, 0, k * P:(k + 1) * P], w_raw[:, k, :], ident[:, :])
            t_.transpose(psX[:, 0:E], wg_raw[:, :], ident[0:E, 0:E]).then_inc(s_wt, 1)
            pe.wait_ge(s_wts, 3)

            def scores(b, i, par, off, m, G):
                h, q = use(i, par, off)
                if m == 0:
                    pe.wait_ge(s_pack[q], DMA * 2 * len(Q_PARTS) * (h + 1))
                ge(pe, s_exp, G - 1)
                qc, h0 = group_of(m)
                for j in range(2):
                    ins = t_.matmul(psS[:, m % 2, j * N:(j + 1) * N], qp[:, q, h0 + j, qc * P:(qc + 1) * P],
                                    kp[:, q, h0 + j, :], start=True, stop=True)
                ins.then_inc(s_s, 1)

            def transposes(b, m):
                G = b * GR + m
                pe.wait_ge(s_exp, G + 1)
                ge(pe, s_mul, G - 1)
                for k in range(4):
                    ins = t_.transpose(psT[:, m % 2, k * P:(k + 1) * P], ex[:, m % 2, k * P:(k + 1) * P], ident[:, :])
                ins.then_inc(s_t, 1)

            def values(b, q, m, G):
                if m == 0:
                    pe.wait_ge(s_v, b + 1)
                    ge(pe, s_o, b)
                pe.wait_ge(s_mul, G + 1)
                qc, h0 = group_of(m)
                col = (qc * (HEADS // HG) + h0 // HG) * P
                for j in range(2):
                    r = VW * ((h0 + j) % HG)
                    for c in range(NC):
                        ins = t_.matmul(psO[r:r + VW, col:col + P], vaug[:, q, c, h0 + j, :],
                                        pT[:, m % 2, (j * NC + c) * P:(j * NC + c + 1) * P],
                                        start=(c == 0), stop=(c == NC - 1))
                ins.then_inc(s_av, 1)

            def body(b, i, par):
                for m in range(GR):
                    if has(b, 0, NB):
                        transposes(b, m)
                    if m + 2 < GR and has(b, 0, NB):
                        scores(b, i, par, 0, m + 2, b * GR + (m + 2))
                    if m + 2 >= GR and has(b, 1, NB):
                        scores(b, i, par, 1, m + 2 - GR, b * GR + (m + 2))
                    if m == 0 and has(b, -1, NB):
                        values(b - 1, (par + 1) % 2, GR - 1, b * GR - 1)
                    if m > 0 and has(b, 0, NB):
                        values(b, par, m - 1, b * GR + (m - 1))
                    if m == 0 and has(b, 2, NB):
                        _, q = use(i, par, 2)
                        pe.wait_ge(s_xn, b + 3)
                        ge(pe, s_xT, b + 2)
                        for c in range(NC):
                            ins = t_.transpose(psX[:, c * P:(c + 1) * P], xn[:, q, c * D:(c + 1) * D], ident[:, :])
                        ins.then_inc(s_xTp, 1)
                    if m == 1 and has(b, 2, NB):
                        _, q = use(i, par, 2)
                        pe.wait_ge(s_xT, b + 3)
                        ge(pe, s_a, b + 1)
                        for k in range(2):
                            ins = t_.matmul(psQ[:, k * N:(k + 1) * N], wT[:, k, :], xT[:, q, :], start=True, stop=True)
                        ins.then_inc(s_qkp, 1)
                    if m == 1 and has(b, -2, NB):
                        pe.wait_ge(s_top, b - 1)
                        o = N + 32
                        for c in range(NC):
                            t_.matmul(psR[:, o + c * E:o + (c + 1) * E], before[:, :], member[:, c, :],
                                      start=True, stop=(c == 0))
                            for c0 in range(c):
                                t_.matmul(psR[:, o + c * E:o + (c + 1) * E], ones_bf[:, :], member[:, c0, :],
                                          start=False, stop=(c0 == c - 1))
                        for c in range(NC):
                            ins = t_.matmul(psR[:, o + NC * E:o + NC * E + E], ones_bf[:, :], member[:, c, :],
                                            start=(c == 0), stop=(c == NC - 1))
                        ins.then_inc(s_rank, 1)
                    if m == 2 and has(b, -1, NB):
                        pe.wait_ge(s_o, b)
                        ge(pe, s_pos, b - 1)
                        for k in range(4):
                            ins = t_.transpose(psR[:, k * P:(k + 1) * P], o_sb[:, k * P:(k + 1) * P], ident[:, :])
                        ins.then_inc(s_otp, 1)
                    if m == 3 and has(b, 1, NB):
                        _, q = use(i, par, 1)
                        ge(pe, s_v, b + 1)
                        pe.wait_ge(s_xT, b + 2)
                        for c in range(NC):
                            ins = t_.matmul(psX[:, N + c * P:N + (c + 1) * P], xT[:, q, c * P:(c + 1) * P],
                                            wT[:, 2, :], start=True, stop=True)
                        ins.then_inc(s_vp, 1)
                    if m == 3 and has(b, -1, NB):
                        pe.wait_ge(s_on, b)
                        for c in range(NC):
                            ins = t_.transpose(psR[:, c * P:(c + 1) * P], on[:, c * D:(c + 1) * D], ident[:, :])
                        ins.then_inc(s_ontp, 1)
                    if m == 4 and has(b, 1, NB):
                        h, q = use(i, par, 1)
                        pe.wait_ge(s_adjin[q], DMA * (h + 1))
                        ge(pe, s_qk, b + 3 if has(b, 2, NB) else b + 2)
                        for c in range(NC):
                            for c0 in range(NC):
                                ins = t_.transpose(psQ[:, c * N + c0 * P:c * N + (c0 + 1) * P],
                                                   adj_in[:, q, c0 * N + c * P:c0 * N + (c + 1) * P], ident[:, :])
                        ins.then_inc(s_ap, 1)
                    if m == 4 and has(b, -1, NB):
                        pe.wait_ge(s_ont, b)
                        for c in range(NC):
                            ins = t_.matmul(psR[:, N + c * P:N + (c + 1) * P], onT[:, c * P:(c + 1) * P],
                                            wT[:, 3, :], start=True, stop=True)
                        ins.then_inc(s_y, 1)
                    if m == 6 and has(b, -1, NB):
                        _, q = use(i, par, -1)
                        pe.wait_ge(s_x2, b)
                        for c in range(NC):
                            ins = t_.transpose(psR[:, c * P:(c + 1) * P], rows[:, q, c, 0, 0:D], ident[:, :])
                        ins.then_inc(s_x2tp, 1)
                    if m == 7 and has(b, -1, NB):
                        pe.wait_ge(s_x2t, b)
                        for c in range(NC):
                            ins = t_.matmul(psR[:, N + c * E:N + (c + 1) * E], x2T[:, c * P:(c + 1) * P],
                                            wgT[:, :], start=True, stop=True)
                        ins.then_inc(s_gate, 1)

            batches(pe, body)

            for e in range(E):
                pe.wait_ge(s_wl[e % WR], DMA * 2 * (e // WR + 1))
                ge(pe, s_w1, e - 1)
                for c in range(FC):
                    ins = t_.transpose(psS[:, e % 2, c * P:(c + 1) * P], w1_raw[:, e % WR, c * D:(c + 1) * D], ident[:, :])
                ins.then_inc(s_wp, 1)
                ge(pe, s_w2, e - 1)
                for c in range(FC):
                    ins = t_.transpose(psT[:, e % 2, c * P:(c + 1) * P], w2_raw[:, e % WR, c * P:(c + 1) * P], ident[:, :])
                ins.then_inc(s_wp, 1)
            pe.wait_ge(s_w1, E)
            pe.wait_ge(s_w2, E)
            pe.wait_ge(s_tab, 1)

            expert = Experts(pe, tab_e)

            def body(t, i, u):
                if has(t, 2, NTILES):
                    w, r = u % 2, (u + 2) % 4
                    pe.wait_ge(f_in[r], DMA * (i + (u + 2) // 4 + 1))
                    ge(pe, f_xT, t + 1)
                    t_.transpose((psX, psO)[w][:, 0:P], xr[:, r, 0:D], ident[:, :]).then_inc(f_xp, 1)
                if has(t, 1, NTILES):
                    w = (u + 1) % 2
                    e = expert(t, i, u, 1)
                    pe.wait_ge(f_xT, t + 2)
                    ge(pe, f_hb, t)
                    t_.matmul(psS[:, w, :], xrT[:, w, :], w1T[:, ds(e * F, F)], start=True, stop=True).then_inc(f_h, 1)
                if has(t, 0, NTILES):
                    w = u % 2
                    pe.wait_ge(f_hb, t + 1)
                    ge(pe, f_hT, t - 1)
                    for c in range(FC):
                        ins = t_.transpose(psT[:, w, c * P:(c + 1) * P], hb[:, w, c * P:(c + 1) * P], ident[:, :])
                    ins.then_inc(f_hp, 1)
                if has(t, -1, NTILES):
                    w = (u - 1) % 2
                    e = expert(t, i, u, -1)
                    ps = psQ if w == 0 else psR
                    pe.wait_ge(f_hT, t)
                    ge(pe, f_yw, t - 2)
                    for c in range(FC):
                        ins = t_.matmul(ps[:, 0:D], hT[:, w, c * P:(c + 1) * P],
                                        w2T[:, ds(e * (FC * D) + c * D, D)], start=(c == 0), stop=(c == FC - 1))
                    ins.then_inc(f_y, 1)

            tiles(pe, body)


_INS = ["x", "adj", "L0_gnn_Wq", "L0_gnn_Wk", "L0_gnn_Wv", "L0_gnn_Wo", "L0_gnn_bo", "L0_ffn_Wg", "L0_ffn_bg",
        "L0_ffn_W1", "L0_ffn_b1", "L0_ffn_W2", "L0_ffn_b2"]


def kernel(**inputs):
    import numpy as _np
    import concourse.bacc as _bacc
    from concourse import mybir as _mybir
    from concourse.bass_utils import run_bass_kernel_spmd as _run

    nc = _bacc.Bacc("TRN2", target_bir_lowering=False, num_devices=1)
    arrays, args = {}, []
    for name in _INS:
        a = _np.ascontiguousarray(inputs[name])
        arrays[f"in_{name}"] = a
        args.append(nc.dram_tensor(f"in_{name}", a.shape, _mybir.dt.from_np(a.dtype), kind="ExternalInput").ap())
    x = arrays["in_x"]
    out = nc.dram_tensor("out_0", x.shape, _mybir.dt.from_np(x.dtype), kind="ExternalOutput").ap()
    adj_moe_kernel(nc, *args, out)
    r = _run(nc, [arrays], core_ids=[0])
    return r.results[0]["out_0"]
```

```python
from contextlib import ExitStack

import concourse.bass as bass
from concourse import mybir

P = 128
F32 = mybir.dt.float32
BF16 = mybir.dt.bfloat16
U32 = mybir.dt.uint32
I32 = mybir.dt.int32
ALU = mybir.AluOpType
ACT = mybir.ActivationFunctionType
AX = mybir.AxisListType
ds = bass.ds

HEADS = 8
SLOTS = 2
LN_EPS = 1e-5
ADJ_EPS = 1e-6
PARTS = 3
Q_PARTS = (0, 1, 2, 0, 1, 0)
K_PARTS = (0, 0, 0, 1, 1, 2)
DMA = 16


def wait_apart(eng, waited, sem, value):
    if isinstance(value, int):
        if value > 0:
            eng.wait_ge(sem, value)
        return
    eng.wait_ge(sem, value)
    eng.sem_inc(waited, 1)


class Chain:

    def __init__(self, eng, sem, waited):
        self.eng, self.sem, self.waited = eng, sem, waited
        self.n, self.i, self.per, self.k = 0, None, 0, 0

    def enter(self, i, per):
        self.i, self.per, self.k = i, per, 0

    def leave(self, times):
        assert self.k == self.per, (self.k, self.per)
        self.n += times * self.per
        self.i, self.k = None, 0

    def value(self):
        return self.n + self.k if self.i is None else self.i * self.per + (self.n + self.k)

    def count(self, ins):
        ins.then_inc(self.sem, 1)
        self.k += 1
        if self.i is None:
            self.n, self.k = self.n + 1, 0

    def after(self):
        self.eng.wait_ge(self.sem, self.value())

    def after_apart(self):
        wait_apart(self.eng, self.waited, self.sem, self.value())

    def __call__(self, ins):
        self.count(ins)
        self.after()


class Experts:

    def __init__(self, eng, table):
        self.eng, self.table = eng, table
        self.ahead = eng.alloc_register("word_ahead")
        eng.reg_load(self.ahead, table[0:1, 0:1])

    def take(self):
        self.word = self.eng.snap(self.ahead, min_val=0, max_val=2 ** 18 - 1)

    def load_next(self, i):
        at = self.table[0:1, i + 2:i + 3] if isinstance(i, int) else self.table[0:1, ds(i + 2, 1)]
        self.eng.reg_load(self.ahead, at)

    def __call__(self, u, off):
        return (self.word >> (3 * (u + off + 1))) & 7


def adj_moe_kernel(nc, x, adj, Wq, Wk, Wv, Wo, bo, Wg, bg, W1, b1, W2, b2, out):
    NB, N, D = x.shape
    E, F, _ = W1.shape
    HD = D // HEADS
    NC = N // P
    NT = NB * NC
    T = NT * P
    FC = F // P
    HG = 4
    VW = P // HG
    GR = NC * HEADS // 2
    KS = len(Q_PARTS) * HD
    ROW = D + 2
    CAP = T + P
    NTILES = (SLOTS * T + E * (P - 1)) // P
    NTILES += -NTILES % 4
    SURPLUS = NTILES - SLOTS * T // P
    WORDS = NTILES // 4 + 2
    PADS = E + SURPLUS
    CG = 4
    assert D == P and N == 2 * P and GR == E == 8 and NB % 2 == 0 and FC == 4

    xs = nc.dram_tensor("routed_rows", [E * CAP + SURPLUS * P, ROW], F32, kind="Internal").ap()
    ys = nc.dram_tensor("slot_results", [SLOTS * T + PADS * P, D], F32, kind="Internal").ap()
    parts_dram = nc.dram_tensor("qk_parts", [2, P, PARTS, 2 * N], BF16, kind="Internal").ap()

    x_v = x.rearrange("b (c p) d -> b p c d", p=P)
    adj_v = adj.rearrange("b (c p) k -> b p c k", p=P)
    out_v = out.rearrange("b (c p) d -> p (b c) d", p=P)

    with ExitStack() as ctx:
        def sb(name, shape, dt=F32):
            return ctx.enter_context(nc.sbuf_tensor(name, shape, dt))

        def sem(name):
            return ctx.enter_context(nc.semaphore(name))

        psS = ctx.enter_context(nc.psum_tensor("psS", [P, 2, 512], F32))
        psT = ctx.enter_context(nc.psum_tensor("psT", [P, 2, 512], F32))
        psO = ctx.enter_context(nc.psum_tensor("psO", [P, 512], F32))
        psX = ctx.enter_context(nc.psum_tensor("psX", [P, 512], F32))
        psQ = ctx.enter_context(nc.psum_tensor("psQ", [P, 512], F32))
        psR = ctx.enter_context(nc.psum_tensor("psR", [P, 512], F32))

        ident = sb("ident", [P, P])
        before = sb("before", [P, P], BF16)
        ones_bf = sb("ones_bf", [P, P], BF16)
        neg_half = sb("neg_half", [P, 2])
        minus1 = sb("minus1", [P, 2])
        adj_eps = sb("adj_eps", [P, 1])
        iota_e = sb("iota_e", [P, E])
        w_raw = sb("w_raw", [P, 4, P])
        wT = sb("wT", [P, 4, P])
        wg_raw = sb("wg_raw", [E, D])
        wgT = sb("wgT", [P, E])
        bo_bc = sb("bo_bc", [P, D])
        bg_bc = sb("bg_bc", [P, E])
        b1_bc = sb("b1_bc", [P, E * F])
        b2_bc = sb("b2_bc", [P, E * D])
        w1_raw = sb("w1_raw", [P, E, FC * D])
        w2_raw = sb("w2_raw", [P, E, F])
        w1T = sb("w1T", [P, E * F])
        w2T = sb("w2T", [P, E * FC * D])

        xin = sb("xin", [P, 2, NC * D])
        adj_in = sb("adj_in", [P, 2, NC * N])
        x1 = sb("x1", [P, NT * D])
        stats = sb("stats", [P, NC, 6])
        mv = sb("mv", [P, 2, NC, 2])
        rstd = sb("rstd", [P, 2, NC])
        shift = sb("shift", [P, 2, NC])
        var_e = sb("var_e", [P, NC])
        xn = sb("xn", [P, 2, NC * D])
        xT = sb("xT", [P, 2, N])
        qk = sb("qk", [P, 2 * N])
        rest = sb("rest", [P, 2 * N])
        parts = sb("parts", [P, 2, PARTS, 2 * N], BF16)
        qp = sb("qp", [KS, 2, HEADS, N], BF16)
        kp = sb("kp", [KS, 2, HEADS, N], BF16)
        vaug = sb("vaug", [P, 2, NC, HEADS, VW])
        adjT = sb("adjT", [P, 2, NC, N])
        nmax = sb("nmax", [P, 4, 2])
        ex = sb("ex", [P, 2, 512])
        pT = sb("pT", [P, 2, 512])
        o_sb = sb("o_sb", [P, 512])
        rec = sb("rec", [P, 16])
        on = sb("on", [P, NC * D])
        onT = sb("onT", [P, NC * D])
        stats2 = sb("stats2", [P, NC, 6])
        mv2 = sb("mv2", [P, NC, 2])
        var2 = sb("var2", [P, NC])
        rstd2 = sb("rstd2", [P, NC])
        shift2 = sb("shift2", [P, NC])
        rows = sb("rows", [P, 2, NC, SLOTS, ROW])
        x2T = sb("x2T", [P, N])
        gate = sb("gate", [P, NC, E])
        top = sb("top", [P, NC, 8])
        topi = sb("topi", [P, NC, 8], U32)
        topf = sb("topf", [P, NC, SLOTS])
        onehot = sb("onehot", [P, NC, SLOTS, E])
        member = sb("member", [P, NC, E], BF16)
        gap = sb("gap", [P, NC])
        egap = sb("egap", [P, NC])
        den2 = sb("den2", [P, NC])
        base = sb("base", [P, E])
        posn = sb("posn", [P, NC, E])
        possel = sb("possel", [P, NC, SLOTS, E])
        posf = sb("posf", [P, NC, SLOTS])
        posi = sb("posi", [P, 2, NC * SLOTS], U32)
        dest = sb("dest", [P, NC, SLOTS])

        padrow = sb("padrow", [P, PADS, ROW])
        end_row = sb("end_row", [1, E], I32)
        ebase = sb("ebase", [P, E])
        cnt_i = sb("cnt_i", [P, E], I32)
        cnt_t = sb("cnt_t", [P, E], I32)
        ntile = sb("ntile", [P, E])
        endt = sb("endt", [P, E])
        iota_t = sb("iota_t", [1, NTILES])
        past = sb("past", [1, NTILES, E])
        pastw = sb("pastw", [1, NTILES, E])
        te = sb("te", [1, NTILES])
        tep = sb("tep", [1, 4 * WORDS + 2])
        tw = sb("tw", [1, NTILES])
        ta = sb("ta", [1, NTILES])
        tb = sb("tb", [1, NTILES])
        packf = sb("packf", [1, WORDS])
        tab_e = sb("tab_e", [1, WORDS], I32)
        tab_row = sb("tab_row", [1, NTILES], I32)

        raw = w1_raw[:, :, :].rearrange("p e f -> p (e f)")

        def carve(start, n, width):
            return raw[:, start:start + n * width].rearrange("p (n w) -> p n w", n=n)

        xr = carve(0, 4, ROW)
        xrT = carve(4 * ROW, 2, P)
        hb = carve(4 * ROW + 2 * P, 2, F)
        hT = carve(4 * ROW + 2 * (P + F), 2, FC * P)
        yb = carve(4 * ROW + 2 * (P + 2 * F), 2, D)
        yw = carve(4 * ROW + 2 * (P + 2 * F + D), 4, D)
        yi = sb("yi", [P, 4], U32)
        yp = sb("yp", [P, 4])

        yin = w1T[:, 0:2 * CG * SLOTS * D].rearrange("p (u c d) -> p u c d", u=2, c=CG)
        ysum = w2T[:, 0:2 * CG * D].rearrange("p (u c d) -> p u c d", u=2, c=CG)

        s_const = sem("s_const")
        s_waited = sem("s_waited")
        s_pc = sem("s_pc")
        s_w = sem("s_w")
        s_wl = sem("s_wl")
        s_b = sem("s_b")
        s_wt = sem("s_wt")
        s_wts = sem("s_wts")
        s_dc = sem("s_dc")
        s_xin = [sem(f"s_xin{p}") for p in range(2)]
        s_adjin = [sem(f"s_adjin{p}") for p in range(2)]
        s_store = [sem(f"s_store{p}") for p in range(2)]
        s_pack = [sem(f"s_pack{p}") for p in range(2)]
        s_ln = sem("s_ln")
        s_rstd = sem("s_rstd")
        s_xn = sem("s_xn")
        s_xb = sem("s_xb")
        s_xTp = sem("s_xTp")
        s_xT = sem("s_xT")
        s_qkp = sem("s_qkp")
        s_qk = sem("s_qk")
        s_parts = sem("s_parts")
        s_vp = sem("s_vp")
        s_v = sem("s_v")
        s_ap = sem("s_ap")
        s_a = sem("s_a")
        s_s = sem("s_s")
        s_max = sem("s_max")
        s_exp = sem("s_exp")
        s_t = sem("s_t")
        s_mul = sem("s_mul")
        s_av = sem("s_av")
        s_o = sem("s_o")
        s_otp = sem("s_otp")
        s_on = sem("s_on")
        s_ontp = sem("s_ontp")
        s_ont = sem("s_ont")
        s_y = sem("s_y")
        s_ln2 = sem("s_ln2")
        s_rstd2 = sem("s_rstd2")
        s_x2 = sem("s_x2")
        s_x2c = sem("s_x2c")
        s_x2tp = sem("s_x2tp")
        s_x2t = sem("s_x2t")
        s_gate = sem("s_gate")
        s_top = sem("s_top")
        s_gexp = sem("s_gexp")
        s_rank = sem("s_rank")
        s_gin = sem("s_gin")
        s_rin = sem("s_rin")
        s_pos = sem("s_pos")
        s_sc = [sem(f"s_sc{p}") for p in range(2)]
        s_pad = sem("s_pad")
        s_padd = sem("s_padd")
        s_sur = sem("s_sur")
        s_tab = sem("s_tab")
        s_ac = sem("s_ac")
        s_w1 = sem("s_w1")
        s_w2 = sem("s_w2")
        s_wp = sem("s_wp")
        f_in = [sem(f"f_in{p}") for p in range(4)]
        f_meta = sem("f_meta")
        f_xp = sem("f_xp")
        f_xT = sem("f_xT")
        f_h = sem("f_h")
        f_hb = sem("f_hb")
        f_hp = sem("f_hp")
        f_hT = sem("f_hT")
        f_y = sem("f_y")
        f_yw = sem("f_yw")
        f_sc = [sem(f"f_sc{p}") for p in range(4)]
        c_in = [sem(f"c_in{p}") for p in range(2)]
        c_add = sem("c_add")
        c_sum = sem("c_sum")
        c_out = sem("c_out")

        block = ctx.enter_context(nc.Block())

        def ge_apart(eng, s, v):
            wait_apart(eng, s_waited, s, v)

        def group_of(m):
            return m // (GR // NC), 2 * (m % (GR // NC))

        def expert_of(b, m):
            return (b - NB) * (GR // 2) + m // 2 if isinstance(b, int) and b in (NB, NB + 1) and m % 2 else None

        def has(v, off, count):
            return not isinstance(v, int) or 0 <= v + off < count

        def ge(eng, s, v):
            if not isinstance(v, int) or v > 0:
                eng.wait_ge(s, v)

        def pipeline(eng, body, lo, first, times, step, hi, chains=()):
            for v in range(lo, first):
                body(v, v // step, v % step)
            with eng.Fori(0, times) as it:
                for chain, per in chains:
                    chain.enter(it, per)
                i = it + first // step
                for u in range(step):
                    body(it * step + (first + u), i, u)
            for chain, _ in chains:
                chain.leave(times)
            for v in range(first + step * times, hi):
                body(v, v // step, v % step)

        def batches(eng, body, chains=()):
            pipeline(eng, body, -4, 4, (NB - 8) // 2, 2, NB + 3, chains)

        def tiles(eng, body, chains=()):
            pipeline(eng, body, -2, 4, NTILES // 4 - 2, 4, NTILES + 1, chains)

        def use(i, par, off):
            return i + (par + off) // 2, (par + off) % 2

        def batch_of(view, b):
            return view[b] if isinstance(b, int) else view[ds(b, 1)].rearrange("o p c d -> (o p) c d")

        def tile_span(t, n):
            return slice(t * D, (t + n) * D) if isinstance(t, int) else ds(t * D, n * D)

        def padding(eng, experts):
            eng.wait_ge(s_pad, 1)
            for e in experts:
                end = eng.value_load(end_row[0:1, e:e + 1], min_val=e * CAP, max_val=e * CAP + T)
                eng.dma_start(xs[ds(end, P)], padrow[:, e, :]).then_inc(s_padd, DMA)

        def chunks(ap):
            return ap.rearrange("p (c d) -> p c d", c=NC)

        @block.sync
        def _(sp):
            for k, w in enumerate((Wq, Wk, Wv, Wo)):
                sp.dma_start(w_raw[:, k, :], w).then_inc(s_w, DMA)
            sp.dma_start(wg_raw[:, :], Wg).then_inc(s_w, DMA)
            sp.dma_start(bo_bc[:, :], bo.unsqueeze(0).broadcast_to([P, D])).then_inc(s_w, DMA)
            sp.dma_start(bg_bc[:, :], bg.unsqueeze(0).broadcast_to([P, E])).then_inc(s_w, DMA)

            def body(b, i, par):
                if has(b, 4, NB):
                    _, q = use(i, par, 4)
                    ge_apart(sp, s_xn, b + 3)
                    ge(sp, s_xb, b + 3)
                    sp.dma_start(chunks(xin[:, q, :]), batch_of(x_v, b + 4)).then_inc(s_xin[q], DMA)
                if has(b, 2, NB):
                    h, q = use(i, par, 2)
                    ge_apart(sp, s_ap, b + 1)
                    sp.dma_start(chunks(adj_in[:, q, :]), batch_of(adj_v, b + 2)).then_inc(s_adjin[q], DMA)
                    ge_apart(sp, s_parts, b + 3)
                    ge(sp, s_pack[q], DMA * 2 * len(Q_PARTS) * h)
                    sp.dma_start(parts_dram[q], parts[:, q, :, :]).then_inc(s_store[q], DMA)
                    ge_apart(sp, s_store[q], DMA * (h + 1))
                    ge_apart(sp, s_s, GR * (b + 1))
                    src = parts_dram[q].rearrange("(h d) s t -> s d h t", h=HEADS)
                    for k in range(len(Q_PARTS)):
                        rows_k = slice(HD * k, HD * (k + 1))
                        sp.dma_start(qp[rows_k, q], src[Q_PARTS[k], :, :, 0:N]).then_inc(s_pack[q], DMA)
                        sp.dma_start(kp[rows_k, q], src[K_PARTS[k], :, :, N:2 * N]).then_inc(s_pack[q], DMA)
                if isinstance(b, int) and b in loads:
                    e = loads.index(b)
                    sp.dma_start(w1_raw[:, e, :].rearrange("p (c d) -> p c d", c=FC),
                                 W1[e].rearrange("(c p) d -> p c d", p=P)).then_inc(s_wl, DMA)
                    sp.dma_start(w2_raw[:, e, :], W2[e]).then_inc(s_wl, DMA)
                    sp.dma_start(b1_bc[:, e * F:(e + 1) * F], b1[e:e + 1].broadcast_to([P, F])).then_inc(s_b, DMA)
                    sp.dma_start(b2_bc[:, e * D:(e + 1) * D], b2[e:e + 1].broadcast_to([P, D])).then_inc(s_b, DMA)

            loads = (-1, 0, 1, 2, 3, NB - 4, NB - 3, NB - 2)
            batches(sp, body)

            padding(sp, range(0, E, 2))

            sp.wait_ge(s_tab, 1)
            sp.wait_ge(s_wp, 2 * E)
            sp.wait_ge(s_padd, DMA * E)
            sp.wait_ge(s_sur, DMA)
            for p in range(2):
                sp.wait_ge(s_sc[p], DMA * NC * SLOTS * (NB // 2))

            def body(t, i, u):
                if has(t, 0, NTILES):
                    first_row = sp.value_load(tab_row[0:1, t:t + 1] if isinstance(t, int) else tab_row[0:1, ds(t, 1)],
                                              min_val=0, max_val=E * CAP + (SURPLUS - 1) * P)
                    ge(sp, f_xp, t - 3)
                    ge_apart(sp, f_meta, t - 3)
                    sp.dma_start(xr[:, u, :], xs[ds(first_row, P)]).then_inc(f_in[u], DMA)

            tiles(sp, body)

            for p in range(4):
                sp.wait_ge(f_sc[p], DMA * (NTILES // 4))
            ys_v = ys[0:SLOTS * T].rearrange("(g c p s) d -> g p c (s d)", c=CG, p=P, s=SLOTS)

            def body(g, i, u):
                ge_apart(sp, c_sum, g - 1)
                sp.dma_start(yin[:, u], ys_v[g] if isinstance(g, int) else
                             ys_v[ds(g, 1)].rearrange("o p c d -> (o p) c d")).then_inc(c_in[u], DMA)

            pipeline(sp, body, 0, 2, NT // CG // 2 - 1, 2, NT // CG)

        @block.gpsimd
        def _(pool):
            g = nc.gpsimd
            link = Chain(pool, s_pc, s_waited)
            link(g.memset(ident[:, :], 1.0))
            link(g.affine_select(out=ident[:, :], in_=ident[:, :], compare_op=ALU.is_equal, fill=0.0,
                                 base=0, pattern=[[-1, P]], channel_multiplier=1))
            link(g.memset(before[:, :], 1.0))
            link(g.affine_select(out=before[:, :], in_=before[:, :], compare_op=ALU.is_gt, fill=0.0,
                                 base=0, pattern=[[1, P]], channel_multiplier=-1))
            link(g.memset(ones_bf[:, :], 1.0))
            link(g.memset(neg_half[:, :], -0.5))
            link(g.memset(minus1[:, :], -1.0))
            link(g.memset(adj_eps[:, :], ADJ_EPS))
            link(g.memset(vaug[:, :, :, :, :], 1.0))
            link(g.memset(padrow[:, :, :], 0.0))
            link(g.iota(padrow[:, :, D:D + 1].rearrange("p e o -> p (e o)"), pattern=[[P, PADS]], base=SLOTS * T,
                        channel_multiplier=1, allow_small_or_imprecise_dtypes=True))
            for tile, pattern, mult in ((iota_e[:, :], [[1, E]], 0), (base[:, :], [[CAP, E]], 0),
                                        (ebase[:, :], [[CAP, E]], 0),
                                        (iota_t[:, :], [[1, NTILES]], 0),
                                        (dest[:, :, :], [[SLOTS * P, NC], [1, SLOTS]], SLOTS)):
                link(g.iota(tile, pattern=pattern, base=0, channel_multiplier=mult,
                            allow_small_or_imprecise_dtypes=True))
            pool.dma_start(xs[E * CAP:E * CAP + SURPLUS * P].rearrange("(k p) r -> p k r", p=P),
                           padrow[:, E:PADS, :]).then_inc(s_sur, DMA)
            pool.sem_inc(s_const, 1)
            pool.wait_ge(s_w, DMA * 7)

            def body(b, i, par):
                if has(b, -3, NB):
                    _, q = use(i, par, -3)
                    ge_apart(pool, s_pos, b - 2)
                    for c in range(NC):
                        for s in range(SLOTS):
                            k = c * SLOTS + s
                            g.indirect_dma_start(xs, bass.IndirectOffsetOnAxis(ap=posi[:, q, k:k + 1], axis=0),
                                                 rows[:, q, c, s, :], None).then_inc(s_sc[q], DMA)
                if has(b, 3, NB):
                    h, q = use(i, par, 3)
                    ge_apart(pool, s_ln, b + 4)
                    link(g.tensor_scalar(var_e[:, :], mv[:, q, :, 1], LN_EPS, None, ALU.add))
                    link(g.tensor_tensor(rstd[:, q, :], var_e[:, :], neg_half[:, :], ALU.pow))
                    link(g.tensor_tensor(shift[:, q, :], mv[:, q, :, 0], rstd[:, q, :], ALU.mult))
                    g.tensor_tensor(shift[:, q, :], shift[:, q, :], minus1[:, :], ALU.mult).then_inc(s_rstd, 1)
                    pool.wait_ge(s_xin[q], DMA * (h + 1))
                    g.tensor_tensor(chunks(x1[:, tile_span((b + 3) * NC, NC)]), chunks(xin[:, q, :]),
                                    bo_bc[:, :].unsqueeze(1).broadcast_to([P, NC, D]), ALU.add).then_inc(s_xb, 1)
                if has(b, 2, NB):
                    h, q = use(i, par, 2)
                    pool.wait_ge(s_qk, b + 3)
                    link.count(g.tensor_tensor(rest[:, :], qk[:, :], parts[:, q, 0, :], ALU.subtract))
                    link(g.tensor_tensor(parts[:, q, 1, :], qk[:, :], parts[:, q, 0, :], ALU.subtract))
                    g.tensor_tensor(parts[:, q, 2, :], rest[:, :], parts[:, q, 1, :],
                                    ALU.subtract).then_inc(s_parts, 1)
                if has(b, -1, NB):
                    ge_apart(pool, s_ln2, b)
                    ge_apart(pool, s_x2, b - 1)
                    link(g.tensor_scalar(var2[:, :], mv2[:, :, 1], LN_EPS, None, ALU.add))
                    link(g.tensor_tensor(rstd2[:, :], var2[:, :], neg_half[:, :], ALU.pow))
                    link(g.tensor_tensor(shift2[:, :], mv2[:, :, 0], rstd2[:, :], ALU.mult))
                    g.tensor_tensor(shift2[:, :], shift2[:, :], minus1[:, :], ALU.mult).then_inc(s_rstd2, 1)

            batches(pool, body, [(link, 16)])
            def body(t, i, u):
                if has(t, -1, NTILES):
                    v = (u - 1) % 4
                    ge_apart(pool, f_yw, t)
                    g.indirect_dma_start(ys, bass.IndirectOffsetOnAxis(ap=yi[:, v:v + 1], axis=0),
                                         yw[:, v, :], None).then_inc(f_sc[v], DMA)

            tiles(pool, body)

        @block.scalar
        def _(act):
            s = nc.scalar
            act.wait_ge(s_const, 1)

            def exps(b, m, G):
                act.wait_ge(s_max, G + 1)
                ge(act, s_t, G - 1)
                for j in range(2):
                    ins = s.activation(ex[:, m % 2, j * N:(j + 1) * N], psS[:, m % 2, j * N:(j + 1) * N],
                                       ACT.Exp, bias=nmax[:, m % 4, j:j + 1])
                ins.then_inc(s_exp, 1)

            def body(b, i, par):
                for m in range(GR):
                    if m + 2 < GR and has(b, 0, NB) or m + 2 >= GR and has(b, 1, NB):
                        exps(b, (m + 2) % GR, b * GR + (m + 2))
                    if m == 0 and has(b, -1, NB):
                        act.wait_ge(s_av, GR * b)
                        s.activation(o_sb[:, :], psO[:, :], ACT.Copy).then_inc(s_o, 1)
                    if m == 0 and has(b, 2, NB):
                        _, q = use(i, par, 2)
                        act.wait_ge(s_xTp, b + 3)
                        s.activation(xT[:, q, :], psX[:, 0:N], ACT.Copy).then_inc(s_xT, 1)
                    if m == 0 and has(b, -2, NB):
                        h, q = use(i, par, -2)
                        act.wait_ge(s_rstd2, b - 1)
                        ge(act, s_sc[q], DMA * NC * SLOTS * h)
                        for c in range(NC):
                            ins = s.activation(rows[:, q, c, 0, 0:D], x1[:, tile_span((b - 2) * NC + c, 1)],
                                               ACT.Identity, bias=shift2[:, c:c + 1], scale=rstd2[:, c:c + 1])
                        ins.then_inc(s_x2, 1)
                    if m == 1 and has(b, 2, NB):
                        act.wait_ge(s_qkp, b + 3)
                        ge(act, s_parts, b + 2)
                        s.activation(qk[:, :], psQ[:, :], ACT.Copy).then_inc(s_ac, 1)
                    if m == 1 and has(b, -2, NB):
                        act.wait_ge(s_x2tp, b - 1)
                        s.activation(x2T[:, :], psX[:, 0:N], ACT.Copy).then_inc(s_x2t, 1)
                    if m == 2 and has(b, 2, NB):
                        h, q = use(i, par, 2)
                        ge(act, s_store[q], DMA * h)
                        s.activation(parts[:, q, 0, :], psQ[:, :], ACT.Copy).then_inc(s_qk, 1)
                    if m == 2 and has(b, -2, NB):
                        _, q = use(i, par, -2)
                        act.wait_ge(s_x2, b - 1)
                        s.activation(rows[:, q, :, 1, 0:D], rows[:, q, :, 0, 0:D], ACT.Copy).then_inc(s_x2c, 1)
                    if m == 4 and has(b, -1, NB):
                        act.wait_ge(s_ontp, b)
                        s.activation(onT[:, :], psR[:, 0:N], ACT.Copy).then_inc(s_ont, 1)
                    if m == 4 and has(b, 1, NB):
                        _, q = use(i, par, 1)
                        act.wait_ge(s_vp, b + 2)
                        ge(act, s_av, GR * b)
                        s.activation(vaug[:, q, :, :, 0:HD],
                                     psX[:, 0:N].rearrange("p (c h d) -> p c h d", c=NC, h=HEADS),
                                     ACT.Copy).then_inc(s_v, 1)
                    if m == 5 and has(b, 1, NB):
                        _, q = use(i, par, 1)
                        act.wait_ge(s_ap, b + 2)
                        ge(act, s_mul, GR * b)
                        s.activation(adjT[:, q, :, :], psQ[:, :].rearrange("p (c k) -> p c k", c=NC),
                                     ACT.Identity, bias=adj_eps[:, 0:1]).then_inc(s_a, 1)
                    if m == 5 and has(b, -2, NB):
                        act.wait_ge(s_top, b - 1)
                        s.activation(egap[:, :], gap[:, :], ACT.Exp).then_inc(s_gexp, 1)
                    if m == 6 and has(b, 3, NB):
                        _, q = use(i, par, 3)
                        act.wait_ge(s_rstd, b + 4)
                        ge(act, s_xTp, b + 2)
                        for c in range(NC):
                            ins = s.activation(xn[:, q, c * D:(c + 1) * D], xin[:, q, c * D:(c + 1) * D], ACT.Identity,
                                               bias=shift[:, q, c:c + 1], scale=rstd[:, q, c:c + 1])
                        ins.then_inc(s_xn, 1)
                    e = expert_of(b, m)
                    if e is not None:
                        act.wait_ge(s_wp, 2 * e + 2)
                        s.activation(w2T[:, e * FC * D:(e + 1) * FC * D], psT[:, e % 2, :], ACT.Copy).then_inc(s_w2, 1)

            batches(act, body)
            padding(act, range(1, E, 2))

            def body(t, i, u):
                if has(t, 2, NTILES):
                    act.wait_ge(f_xp, t + 3)
                    ge(act, f_h, t + 1)
                    s.activation(xrT[:, u % 2, :], (psX, psO)[u % 2][:, 0:P], ACT.Copy).then_inc(f_xT, 1)
                if has(t, 0, NTILES):
                    act.wait_ge(f_hp, t + 1)
                    ge(act, f_y, t - 1)
                    s.activation(hT[:, u % 2, :], psT[:, u % 2, :], ACT.Relu).then_inc(f_hT, 1)

            tiles(act, body)

            def body(g, i, u):
                act.wait_ge(c_sum, g + 1)
                src = x1[:, tile_span(g * CG, CG)].rearrange("p (c d) -> p c d", c=CG)
                dst = out_v[:, g * CG:(g + 1) * CG, :] if isinstance(g, int) else out_v[:, ds(g * CG, CG), :]
                act.dma_start(dst, src).then_inc(c_out, DMA)

            pipeline(act, body, 0, 2, NT // CG // 2 - 1, 2, NT // CG)
            act.wait_ge(c_out, DMA * (NT // CG))

        @block.vector
        def _(dve):
            v = nc.vector
            link = Chain(dve, s_dc, s_waited)
            dve.wait_ge(s_wt, 1)
            v.tensor_scalar(wT[:, 0, :], psS[:, 0, 0:P], float(HD) ** -0.5, None, ALU.mult).then_inc(s_wts, 1)
            v.tensor_copy(wT[:, 1:4, :].rearrange("p k o -> p (k o)"), psS[:, 0, P:4 * P]).then_inc(s_wts, 1)
            v.tensor_copy(wgT[:, :], psX[:, 0:E]).then_inc(s_wts, 1)
            dve.wait_ge(s_const, 1)
            dve.wait_ge(s_w, DMA * 7)

            def body(b, i, par):
                for m in range(GR):
                    end, last, tail, front = has(b, -3, NB), has(b, -2, NB), has(b, -1, NB), has(b, 3, NB)
                    _, qe = use(i, par, -3)
                    _, q2 = use(i, par, -2)
                    h3, q3 = use(i, par, 3)
                    G = b * GR + m
                    if m + 2 < GR and has(b, 0, NB) or m + 2 >= GR and has(b, 1, NB):
                        dve.wait_ge(s_s, G + 3)
                        v.tensor_reduce(nmax[:, (m + 2) % 4, :], psS[:, m % 2, :].rearrange("p (j k) -> p j k", j=2),
                                        AX.X, ALU.max, negate=True).then_inc(s_max, 1)

                    if m == 0 and end:
                        link.after()
                        link.count(v.tensor_reduce(posf[:, :, :], possel[:, :, :, :], AX.X, ALU.add))
                        link.count(v.tensor_tensor(rows[:, qe, :, 1, D + 1:D + 2], rows[:, qe, :, 0, D + 1:D + 2],
                                                   egap[:, :].unsqueeze(2), ALU.mult))
                    if m == 0 and front:
                        ge_apart(dve, s_ln, b + 3)
                        ge_apart(dve, s_xin[q3], DMA * (h3 + 1))
                        for c in range(NC):
                            link.count(v.bn_stats(stats[:, c, :], xin[:, q3, c * D:(c + 1) * D]))
                    if m == 3 and last:
                        ge_apart(dve, s_gin, b - 1)
                        for c in range(NC):
                            link.count(v.max(top[:, c, :], gate[:, c, :]))
                    if m == 3 and tail:
                        link.after()
                        v.tensor_tensor(on[:, :].rearrange("p (k d) -> p k d", d=HD),
                                        psR[:, :].rearrange("p (k w) -> p k w", w=VW)[:, :, 0:HD],
                                        rec[:, :].unsqueeze(2).broadcast_to([P, 16, HD]), ALU.mult).then_inc(s_on, 1)
                    if m == 4 and last:
                        link.after()
                        link.count(v.tensor_copy(topf[:, :, :], topi[:, :, 0:SLOTS]))
                    if m == 5 and last:
                        link.after()
                        v.tensor_tensor(member[:, :, :], onehot[:, :, 0, :], onehot[:, :, 1, :],
                                        ALU.add).then_inc(s_top, 1)
                    if m == 6 and tail:
                        link.after_apart()
                        for c in range(NC):
                            link.count(v.bn_stats(stats2[:, c, :], x1[:, tile_span((b - 1) * NC + c, 1)]))
                    if m == 7 and last:
                        link.after()
                        v.tensor_tensor(base[:, :], psX[:, NC * E:(NC + 1) * E], base[:, :], ALU.add).then_inc(s_rin, 1)
                        dve.wait_ge(s_gexp, b - 1)
                        link.count(v.tensor_scalar(den2[:, :], egap[:, :], 1.0, None, ALU.add))
                        link.count(v.tensor_copy(rows[:, q2, :, :, D:D + 1], dest[:, :, :].unsqueeze(3)))

                    if has(b, 0, NB):
                        qc, _ = group_of(m)
                        if m == 0:
                            dve.wait_ge(s_a, b + 1)
                        dve.wait_ge(s_t, G + 1)
                        ge(dve, s_av, G - 1)
                        v.tensor_tensor(pT[:, m % 2, :].rearrange("p (j c q) -> p j c q", j=2, c=NC),
                                        psT[:, m % 2, :].rearrange("p (j c q) -> p j c q", j=2, c=NC),
                                        adjT[:, par, :, qc * P:(qc + 1) * P].unsqueeze(1)
                                        .broadcast_to([P, 2, NC, P]), ALU.mult).then_inc(s_mul, 1)

                    if m == 0 and end:
                        link.after()
                        dve.wait_ge(s_x2c, b - 2)
                        v.tensor_copy(posi[:, qe, :], posf[:, :, :].rearrange("p c s -> p (c s)")).then_inc(s_pos, 1)
                    if m == 0 and front:
                        link.after_apart()
                        for c in range(NC):
                            ins = v.bn_aggr(mv[:, q3, c, :], stats[:, c, :])
                            if c < NC - 1:
                                link.count(ins)
                        ins.then_inc(s_ln, 1)
                    if m == 2 and last:
                        dve.wait_ge(s_gate, b - 1)
                        v.tensor_tensor(gate[:, :, :], psX[:, 0:NC * E].rearrange("p (c e) -> p c e", c=NC),
                                        bg_bc[:, :].unsqueeze(1).broadcast_to([P, NC, E]), ALU.add).then_inc(s_gin, 1)
                    if m == 2 and tail:
                        dve.wait_ge(s_otp, b)
                        link.count(v.reciprocal(rec[:, :].unsqueeze(2),
                                                psR[:, :].rearrange("p (k w) -> p k w", w=VW)[:, :, HD:HD + 1]))
                    if m == 3 and last:
                        link.after_apart()
                        for c in range(NC):
                            link.count(v.max_index(topi[:, c, :], top[:, c, :], gate[:, c, :]))
                    if m == 4 and last:
                        link.after()
                        link.count(v.tensor_tensor(
                            onehot[:, :, :, :], iota_e[:, :].unsqueeze(1).unsqueeze(1).broadcast_to([P, NC, SLOTS, E]),
                            topf[:, :, :].unsqueeze(3).broadcast_to([P, NC, SLOTS, E]), ALU.is_equal))
                        link.count(v.tensor_tensor(gap[:, :], top[:, :, 1], top[:, :, 0], ALU.subtract))
                    if m == 5 and tail:
                        dve.wait_ge(s_y, b)
                        dve.wait_ge(s_xb, b)
                        x1_b = x1[:, tile_span((b - 1) * NC, NC)]
                        link.count(v.tensor_tensor(x1_b, psR[:, N:2 * N], x1_b, ALU.add))
                    if m == 6 and tail:
                        link.after_apart()
                        for c in range(NC):
                            ins = v.bn_aggr(mv2[:, c, :], stats2[:, c, :])
                            if c < NC - 1:
                                link.count(ins)
                        ins.then_inc(s_ln2, 1)
                    if m == 6 and last:
                        dve.wait_ge(s_rank, b - 1)
                        ge(dve, s_rin, b - 2)
                        link.count(v.tensor_tensor(posn[:, :, :], psX[:, 0:NC * E].rearrange("p (c e) -> p c e", c=NC),
                                                   base[:, :].unsqueeze(1).broadcast_to([P, NC, E]), ALU.add))
                    if m == 7 and last:
                        link.after()
                        link.count(v.tensor_tensor(possel[:, :, :, :], onehot[:, :, :, :],
                                                   posn[:, :, :].unsqueeze(2).broadcast_to([P, NC, SLOTS, E]), ALU.mult))
                        link.count(v.reciprocal(rows[:, q2, :, 0, D + 1:D + 2], den2[:, :].unsqueeze(2)))
                        link.count(v.tensor_scalar(dest[:, :, :], dest[:, :, :], float(SLOTS * N), None, ALU.add))
                    e = expert_of(b, m)
                    if e is not None:
                        dve.wait_ge(s_wp, 2 * e + 1)
                        v.tensor_copy(w1T[:, e * F:(e + 1) * F], psS[:, e % 2, :]).then_inc(s_w1, 1)

            batches(dve, body, [(link, 2 * 23)])

            dve.wait_ge(s_rin, NB)
            v.tensor_copy(end_row[:, :], base[0:1, :]).then_inc(s_pad, 1)
            link(v.tensor_tensor(ntile[:, :], base[:, :], ebase[:, :], ALU.subtract))
            link(v.tensor_scalar(cnt_i[:, :], ntile[:, :], float(P - 1), None, ALU.add))
            link(v.tensor_scalar(cnt_t[:, :], cnt_i[:, :], 7, None, ALU.arith_shift_right))
            link(v.tensor_copy(ntile[:, :], cnt_t[:, :]))
            link(v.tensor_copy(endt[:, :], ntile[:, :]))
            for e in range(1, E):
                link(v.tensor_tensor(endt[:, e:e + 1], endt[:, e:e + 1], endt[:, e - 1:e], ALU.add))
            link(v.tensor_tensor(past[:, :, :], iota_t[:, :].unsqueeze(2).broadcast_to([1, NTILES, E]),
                                 endt[0:1, :].unsqueeze(1).broadcast_to([1, NTILES, E]), ALU.is_ge))
            link(v.tensor_reduce(te[:, :], past[:, :, :], AX.X, ALU.add))
            link(v.tensor_tensor(pastw[:, :, :], past[:, :, :],
                                 ntile[0:1, :].unsqueeze(1).broadcast_to([1, NTILES, E]), ALU.mult))
            link(v.tensor_reduce(tw[:, :], pastw[:, :, :], AX.X, ALU.add))
            link(v.tensor_tensor(ta[:, :], iota_t[:, :], tw[:, :], ALU.subtract))
            link(v.memset(tep[:, :], 0.0))
            link(v.tensor_scalar(tep[:, 5:NTILES + 5], te[:, :], float(E - 1), None, ALU.min))
            link(v.memset(packf[:, :], 0.0))
            for k in range(6):
                link(v.scalar_tensor_tensor(out=packf[:, :], in0=tep[:, k:k + 4 * WORDS - 3:4], scalar=float(E ** k),
                                            in1=packf[:, :], op0=ALU.mult, op1=ALU.add))
            link(v.tensor_copy(tab_e[:, :], packf[:, :]))
            link(v.tensor_scalar(tb[:, :], te[:, :], float(CAP), None, ALU.mult))
            v.scalar_tensor_tensor(out=tab_row[:, :], in0=ta[:, :], scalar=float(P), in1=tb[:, :],
                                   op0=ALU.mult, op1=ALU.add).then_inc(s_tab, 1)

            dve.wait_ge(s_b, DMA * 2 * E)
            dve.wait_ge(s_tab, 1)

            expert = Experts(dve, tab_e)

            def body(t, i, u):
                if u == 0 or isinstance(t, int) and t == -2:
                    expert.take()
                if has(t, 1, NTILES):
                    w = (u + 1) % 2
                    e = expert(u, 1)
                    dve.wait_ge(f_h, t + 2)
                    ge(dve, f_hp, t)
                    v.tensor_tensor(hb[:, w, :], psS[:, w, :], b1_bc[:, ds(e * F, F)], ALU.add).then_inc(f_hb, 1)
                if u == 3 and has(t, 1, NTILES + 1):
                    expert.load_next(i)
                if has(t, 1, NTILES):
                    r, n = (u + 1) % 4, i + (u + 1) // 4
                    dve.wait_ge(f_in[r], DMA * (n + 1))
                    ge(dve, f_sc[r], DMA * n)
                    link.count(v.tensor_copy(yi[:, r:r + 1], xr[:, r, D:D + 1]))
                    v.tensor_copy(yp[:, r:r + 1], xr[:, r, D + 1:D + 2]).then_inc(f_meta, 1)
                if has(t, -1, NTILES):
                    w, r = (u - 1) % 2, (u - 1) % 4
                    e = expert(u, -1)
                    dve.wait_ge(f_y, t)
                    ps = psQ if w == 0 else psR
                    link(v.tensor_tensor(yb[:, w, :], ps[:, 0:D], b2_bc[:, ds(e * D, D)], ALU.add))
                    v.tensor_scalar(yw[:, r, :], yb[:, w, :], yp[:, r:r + 1], None,
                                    ALU.mult).then_inc(f_yw, 1)

            tiles(dve, body, [(link, 8)])

            def body(g, i, u):
                dve.wait_ge(c_in[u], DMA * (i + 1))
                link(v.tensor_tensor(ysum[:, u], yin[:, u, :, 0:D], yin[:, u, :, D:2 * D], ALU.add))
                r = x1[:, tile_span(g * CG, CG)]
                v.tensor_tensor(r, ysum[:, u].rearrange("p c d -> p (c d)"), r, ALU.add).then_inc(c_sum, 1)

            pipeline(dve, body, 0, 2, NT // CG // 2 - 1, 2, NT // CG, [(link, 2)])

        @block.tensor
        def _(pe):
            t_ = nc.tensor
            pe.wait_ge(s_w, DMA * 7)
            pe.wait_ge(s_const, 1)
            for k in range(4):
                t_.transpose(psS[:, 0, k * P:(k + 1) * P], w_raw[:, k, :], ident[:, :])
            t_.transpose(psX[:, 0:E], wg_raw[:, :], ident[0:E, 0:E]).then_inc(s_wt, 1)
            pe.wait_ge(s_wts, 3)

            def scores(b, i, par, off, m, G):
                h, q = use(i, par, off)
                if m == 0:
                    pe.wait_ge(s_pack[q], DMA * 2 * len(Q_PARTS) * (h + 1))
                ge(pe, s_exp, G - 1)
                qc, h0 = group_of(m)
                for j in range(2):
                    ins = t_.matmul(psS[:, m % 2, j * N:(j + 1) * N], qp[:, q, h0 + j, qc * P:(qc + 1) * P],
                                    kp[:, q, h0 + j, :], start=True, stop=True)
                ins.then_inc(s_s, 1)

            def transposes(b, m):
                G = b * GR + m
                pe.wait_ge(s_exp, G + 1)
                ge(pe, s_mul, G - 1)
                for k in range(4):
                    ins = t_.transpose(psT[:, m % 2, k * P:(k + 1) * P], ex[:, m % 2, k * P:(k + 1) * P], ident[:, :])
                ins.then_inc(s_t, 1)

            def values(b, q, m, G):
                if m == 0:
                    pe.wait_ge(s_v, b + 1)
                    ge(pe, s_o, b)
                pe.wait_ge(s_mul, G + 1)
                qc, h0 = group_of(m)
                col = (qc * (HEADS // HG) + h0 // HG) * P
                for j in range(2):
                    r = VW * ((h0 + j) % HG)
                    for c in range(NC):
                        ins = t_.matmul(psO[r:r + VW, col:col + P], vaug[:, q, c, h0 + j, :],
                                        pT[:, m % 2, (j * NC + c) * P:(j * NC + c + 1) * P],
                                        start=(c == 0), stop=(c == NC - 1))
                ins.then_inc(s_av, 1)

            def body(b, i, par):
                for m in range(GR):
                    if m + 2 < GR and has(b, 0, NB):
                        scores(b, i, par, 0, m + 2, b * GR + (m + 2))
                    if m + 2 >= GR and has(b, 1, NB):
                        scores(b, i, par, 1, m + 2 - GR, b * GR + (m + 2))
                    if has(b, 0, NB):
                        transposes(b, m)
                    if m == 0 and has(b, -1, NB):
                        values(b - 1, (par + 1) % 2, GR - 1, b * GR - 1)
                    if m > 0 and has(b, 0, NB):
                        values(b, par, m - 1, b * GR + (m - 1))
                    if m == 0 and has(b, 2, NB):
                        _, q = use(i, par, 2)
                        pe.wait_ge(s_xn, b + 3)
                        ge(pe, s_v, b + 1)
                        ge(pe, s_rin, b - 2)
                        for c in range(NC):
                            ins = t_.transpose(psX[:, c * P:(c + 1) * P], xn[:, q, c * D:(c + 1) * D], ident[:, :])
                        ins.then_inc(s_xTp, 1)
                    if m == 1 and has(b, 2, NB):
                        _, q = use(i, par, 2)
                        pe.wait_ge(s_xT, b + 3)
                        ge(pe, s_a, b + 1)
                        for k in range(2):
                            ins = t_.matmul(psQ[:, k * N:(k + 1) * N], wT[:, k, :], xT[:, q, :], start=True, stop=True)
                        ins.then_inc(s_qkp, 1)
                    if m == 1 and has(b, -2, NB):
                        _, q = use(i, par, -2)
                        pe.wait_ge(s_x2, b - 1)
                        ge(pe, s_rin, b - 2)
                        for c in range(NC):
                            ins = t_.transpose(psX[:, c * P:(c + 1) * P], rows[:, q, c, 0, 0:D], ident[:, :])
                        ins.then_inc(s_x2tp, 1)
                    if m == 2 and has(b, -1, NB):
                        pe.wait_ge(s_o, b)
                        ge(pe, s_ln2, b - 1)
                        for k in range(4):
                            ins = t_.transpose(psR[:, k * P:(k + 1) * P], o_sb[:, k * P:(k + 1) * P], ident[:, :])
                        ins.then_inc(s_otp, 1)
                    if m == 2 and has(b, -2, NB):
                        pe.wait_ge(s_x2t, b - 1)
                        for c in range(NC):
                            ins = t_.matmul(psX[:, c * E:(c + 1) * E], x2T[:, c * P:(c + 1) * P],
                                            wgT[:, :], start=True, stop=True)
                        ins.then_inc(s_gate, 1)
                    if m == 4 and has(b, -1, NB):
                        pe.wait_ge(s_on, b)
                        for c in range(NC):
                            ins = t_.transpose(psR[:, c * P:(c + 1) * P], on[:, c * D:(c + 1) * D], ident[:, :])
                        ins.then_inc(s_ontp, 1)
                    if m == 4 and has(b, 1, NB):
                        _, q = use(i, par, 1)
                        pe.wait_ge(s_xT, b + 3 if has(b, 2, NB) else b + 2)
                        ge(pe, s_gin, b - 1)
                        for c in range(NC):
                            ins = t_.matmul(psX[:, c * P:(c + 1) * P], xT[:, q, c * P:(c + 1) * P],
                                            wT[:, 2, :], start=True, stop=True)
                        ins.then_inc(s_vp, 1)
                    if m == 5 and has(b, -1, NB):
                        pe.wait_ge(s_ont, b)
                        for c in range(NC):
                            ins = t_.matmul(psR[:, N + c * P:N + (c + 1) * P], onT[:, c * P:(c + 1) * P],
                                            wT[:, 3, :], start=True, stop=True)
                        ins.then_inc(s_y, 1)
                    if m == 5 and has(b, 1, NB):
                        h, q = use(i, par, 1)
                        pe.wait_ge(s_adjin[q], DMA * (h + 1))
                        ge(pe, s_qk, b + 3 if has(b, 2, NB) else b + 2)
                        for c in range(NC):
                            for c0 in range(NC):
                                ins = t_.transpose(psQ[:, c * N + c0 * P:c * N + (c0 + 1) * P],
                                                   adj_in[:, q, c0 * N + c * P:c0 * N + (c + 1) * P], ident[:, :])
                        ins.then_inc(s_ap, 1)
                    if m == 6 and has(b, -2, NB):
                        pe.wait_ge(s_top, b - 1)
                        if has(b, 1, NB):
                            pe.wait_ge(s_v, b + 2)
                        for c in range(NC):
                            t_.matmul(psX[:, c * E:(c + 1) * E], before[:, :], member[:, c, :],
                                      start=True, stop=(c == 0))
                            for c0 in range(c):
                                t_.matmul(psX[:, c * E:(c + 1) * E], ones_bf[:, :], member[:, c0, :],
                                          start=False, stop=(c0 == c - 1))
                        for c in range(NC):
                            ins = t_.matmul(psX[:, NC * E:(NC + 1) * E], ones_bf[:, :], member[:, c, :],
                                            start=(c == 0), stop=(c == NC - 1))
                        ins.then_inc(s_rank, 1)
                    e = expert_of(b, m)
                    if e is not None:
                        pe.wait_ge(s_wl, DMA * 2 * E)
                        ge(pe, s_w1, e - 1)
                        for c in range(FC):
                            ins = t_.transpose(psS[:, e % 2, c * P:(c + 1) * P], w1_raw[:, e, c * D:(c + 1) * D],
                                               ident[:, :])
                        ins.then_inc(s_wp, 1)
                        ge(pe, s_w2, e - 1)
                        for c in range(FC):
                            ins = t_.transpose(psT[:, e % 2, c * P:(c + 1) * P], w2_raw[:, e, c * P:(c + 1) * P],
                                               ident[:, :])
                        ins.then_inc(s_wp, 1)

            batches(pe, body)

            pe.wait_ge(s_w1, E)
            pe.wait_ge(s_w2, E)
            pe.wait_ge(s_tab, 1)

            expert = Experts(pe, tab_e)

            def body(t, i, u):
                if u == 0 or isinstance(t, int) and t == -2:
                    expert.take()
                if has(t, 2, NTILES):
                    w, r = u % 2, (u + 2) % 4
                    pe.wait_ge(f_in[r], DMA * (i + (u + 2) // 4 + 1))
                    ge(pe, f_xT, t + 1)
                    t_.transpose((psX, psO)[w][:, 0:P], xr[:, r, 0:D], ident[:, :]).then_inc(f_xp, 1)
                if has(t, 1, NTILES):
                    w = (u + 1) % 2
                    e = expert(u, 1)
                    pe.wait_ge(f_xT, t + 2)
                    ge(pe, f_hb, t)
                    t_.matmul(psS[:, w, :], xrT[:, w, :], w1T[:, ds(e * F, F)], start=True, stop=True).then_inc(f_h, 1)
                if u == 3 and has(t, 1, NTILES + 1):
                    expert.load_next(i)
                if has(t, 0, NTILES):
                    w = u % 2
                    pe.wait_ge(f_hb, t + 1)
                    ge(pe, f_hT, t - 1)
                    for c in range(FC):
                        ins = t_.transpose(psT[:, w, c * P:(c + 1) * P], hb[:, w, c * P:(c + 1) * P], ident[:, :])
                    ins.then_inc(f_hp, 1)
                if has(t, -1, NTILES):
                    w = (u - 1) % 2
                    e = expert(u, -1)
                    ps = psQ if w == 0 else psR
                    pe.wait_ge(f_hT, t)
                    ge(pe, f_yw, t - 2)
                    for c in range(FC):
                        ins = t_.matmul(ps[:, 0:D], hT[:, w, c * P:(c + 1) * P],
                                        w2T[:, ds(e * (FC * D) + c * D, D)], start=(c == 0), stop=(c == FC - 1))
                    ins.then_inc(f_y, 1)

            tiles(pe, body)


_INS = ["x", "adj", "L0_gnn_Wq", "L0_gnn_Wk", "L0_gnn_Wv", "L0_gnn_Wo", "L0_gnn_bo", "L0_ffn_Wg", "L0_ffn_bg",
        "L0_ffn_W1", "L0_ffn_b1", "L0_ffn_W2", "L0_ffn_b2"]


def kernel(**inputs):
    import numpy as _np
    import concourse.bacc as _bacc
    from concourse import mybir as _mybir
    from concourse.bass_utils import run_bass_kernel_spmd as _run

    nc = _bacc.Bacc("TRN2", target_bir_lowering=False, num_devices=1)
    arrays, args = {}, []
    for name in _INS:
        a = _np.ascontiguousarray(inputs[name])
        arrays[f"in_{name}"] = a
        args.append(nc.dram_tensor(f"in_{name}", a.shape, _mybir.dt.from_np(a.dtype), kind="ExternalInput").ap())
    x = arrays["in_x"]
    out = nc.dram_tensor("out_0", x.shape, _mybir.dt.from_np(x.dtype), kind="ExternalOutput").ap()
    adj_moe_kernel(nc, *args, out)
    r = _run(nc, [arrays], core_ids=[0])
    return r.results[0]["out_0"]
```

```python
from contextlib import ExitStack

import concourse.bass as bass
from concourse import mybir

P = 128
F32 = mybir.dt.float32
BF16 = mybir.dt.bfloat16
U32 = mybir.dt.uint32
I32 = mybir.dt.int32
ALU = mybir.AluOpType
ACT = mybir.ActivationFunctionType
AX = mybir.AxisListType
ds = bass.ds

HEADS = 8
SLOTS = 2
LN_EPS = 1e-5
ADJ_EPS = 1e-6
PARTS = 3
PRODUCTS = (3, 2, 1)
DMA = 16


def wait_apart(eng, waited, sem, value):
    if isinstance(value, int):
        if value > 0:
            eng.wait_ge(sem, value)
        return
    eng.wait_ge(sem, value)
    eng.sem_inc(waited, 1)


class Chain:

    def __init__(self, eng, sem, waited):
        self.eng, self.sem, self.waited = eng, sem, waited
        self.n, self.i, self.per, self.k = 0, None, 0, 0

    def enter(self, i, per):
        self.i, self.per, self.k = i, per, 0

    def leave(self, times):
        assert self.k == self.per, (self.k, self.per)
        self.n += times * self.per
        self.i, self.k = None, 0

    def value(self):
        return self.n + self.k if self.i is None else self.i * self.per + (self.n + self.k)

    def count(self, ins):
        ins.then_inc(self.sem, 1)
        self.k += 1
        if self.i is None:
            self.n, self.k = self.n + 1, 0

    def after(self):
        self.eng.wait_ge(self.sem, self.value())

    def after_apart(self):
        wait_apart(self.eng, self.waited, self.sem, self.value())

    def __call__(self, ins):
        self.count(ins)
        self.after()


class Experts:

    def __init__(self, eng, table):
        self.eng, self.table = eng, table
        self.ahead = eng.alloc_register("word_ahead")
        eng.reg_load(self.ahead, table[0:1, 0:1])

    def take(self):
        self.word = self.eng.snap(self.ahead, min_val=0, max_val=2 ** 18 - 1)

    def load_next(self, i):
        at = self.table[0:1, i + 2:i + 3] if isinstance(i, int) else self.table[0:1, ds(i + 2, 1)]
        self.eng.reg_load(self.ahead, at)

    def __call__(self, u, off):
        return (self.word >> (3 * (u + off + 1))) & 7


def adj_moe_kernel(nc, x, adj, Wq, Wk, Wv, Wo, bo, Wg, bg, W1, b1, W2, b2, out):
    NB, N, D = x.shape
    E, F, _ = W1.shape
    HD = D // HEADS
    NC = N // P
    NT = NB * NC
    T = NT * P
    FC = F // P
    HG = 4
    VW = P // HG
    GR = NC * HEADS // 2
    KS = sum(PRODUCTS) * HD
    ROW = D + 2
    CAP = T + P
    NTILES = (SLOTS * T + E * (P - 1)) // P
    NTILES += -NTILES % 4
    SURPLUS = NTILES - SLOTS * T // P
    WORDS = NTILES // 4 + 2
    PADS = E + SURPLUS
    CG = 4
    CB = 4
    assert D == P and N == 2 * P and GR == E == 8 and NB % 2 == 0 and FC == 4

    xs = nc.dram_tensor("routed_rows", [E * CAP + SURPLUS * P, ROW], F32, kind="Internal").ap()
    ys = nc.dram_tensor("slot_results", [SLOTS * T + PADS * P, D], F32, kind="Internal").ap()
    parts_dram = nc.dram_tensor("qk_parts", [2, 2 * PARTS, P, N], BF16, kind="Internal").ap()

    x_v = x.rearrange("b (c p) d -> b p c d", p=P)
    adj_v = adj.rearrange("b (c p) k -> b p c k", p=P)
    out_v = out.rearrange("b (c p) d -> p (b c) d", p=P)

    with ExitStack() as ctx:
        def sb(name, shape, dt=F32):
            return ctx.enter_context(nc.sbuf_tensor(name, shape, dt))

        def sem(name):
            return ctx.enter_context(nc.semaphore(name))

        psS = ctx.enter_context(nc.psum_tensor("psS", [P, 2, 512], F32))
        psT = ctx.enter_context(nc.psum_tensor("psT", [P, 2, 512], F32))
        psO = ctx.enter_context(nc.psum_tensor("psO", [P, 512], F32))
        psX = ctx.enter_context(nc.psum_tensor("psX", [P, 512], F32))
        psQ = ctx.enter_context(nc.psum_tensor("psQ", [P, 512], F32))
        psR = ctx.enter_context(nc.psum_tensor("psR", [P, 512], F32))

        ident = sb("ident", [P, P])
        before = sb("before", [P, P], BF16)
        ones_bf = sb("ones_bf", [P, P], BF16)
        neg_half = sb("neg_half", [P, 2])
        minus1 = sb("minus1", [P, 2])
        adj_eps = sb("adj_eps", [P, 1])
        warm = sb("warm", [P, 1])
        iota_e = sb("iota_e", [P, E])
        w_raw = sb("w_raw", [P, 4, P])
        wT = sb("wT", [P, 4, P])
        wg_raw = sb("wg_raw", [E, D])
        wgT = sb("wgT", [P, E])
        bo_bc = sb("bo_bc", [P, D])
        bg_bc = sb("bg_bc", [P, E])
        b1_bc = sb("b1_bc", [P, E * F])
        b2_bc = sb("b2_bc", [P, E * D])
        w1_raw = sb("w1_raw", [P, E, FC * D])
        w2_raw = sb("w2_raw", [P, E, F])
        w1T = sb("w1T", [P, E * F])
        w2T = sb("w2T", [P, E * FC * D])

        xin = sb("xin", [P, 2, NC * D])
        adj_in = sb("adj_in", [P, 2, NC * N])
        x1 = sb("x1", [P, NT * D])
        stats = sb("stats", [P, NC, 6])
        mv = sb("mv", [P, 2, NC, 2])
        rstd = sb("rstd", [P, 2, NC])
        shift = sb("shift", [P, 2, NC])
        var_e = sb("var_e", [P, NC])
        xn = sb("xn", [P, 2, NC * D])
        xT = sb("xT", [P, 2, N])
        qk = sb("qk", [P, 2 * N])
        rest = sb("rest", [P, 2 * N])
        parts = sb("parts", [P, 2, 2 * PARTS, N], BF16)
        qp = sb("qp", [KS, 2, HEADS, N], BF16)
        kp = sb("kp", [KS, 2, HEADS, N], BF16)
        vaug = sb("vaug", [P, 2, NC, HEADS, VW])
        adjT = sb("adjT", [P, 2, NC, N])
        nmax = sb("nmax", [P, 4, 2])
        ex = sb("ex", [P, 2, 512])
        pT = sb("pT", [P, 2, 512])
        o_sb = sb("o_sb", [P, 512])
        rec = sb("rec", [P, 16])
        on = sb("on", [P, NC * D])
        onT = sb("onT", [P, NC * D])
        stats2 = sb("stats2", [P, NC, 6])
        mv2 = sb("mv2", [P, NC, 2])
        var2 = sb("var2", [P, NC])
        rstd2 = sb("rstd2", [P, NC])
        shift2 = sb("shift2", [P, NC])
        rows = sb("rows", [P, 2, NC, SLOTS, ROW])
        x2T = sb("x2T", [P, N])
        gate = sb("gate", [P, NC, E])
        top = sb("top", [P, NC, 8])
        topi = sb("topi", [P, NC, 8], U32)
        onehot = sb("onehot", [P, NC, SLOTS, E], BF16)
        egap = sb("egap", [P, NC])
        den2 = sb("den2", [P, NC])
        base = sb("base", [P, E])
        posn = sb("posn", [P, NC, E])
        possel = sb("possel", [P, NC, SLOTS, E])
        posf = sb("posf", [P, NC, SLOTS])
        posi = sb("posi", [P, 2, NC * SLOTS], U32)

        padrow = sb("padrow", [P, PADS, ROW])
        end_row = sb("end_row", [1, E], I32)
        ebase = sb("ebase", [P, E])
        cnt_i = sb("cnt_i", [P, E], I32)
        cnt_t = sb("cnt_t", [P, E], I32)
        ntile = sb("ntile", [P, E])
        endt = sb("endt", [P, E])
        iota_t = sb("iota_t", [1, NTILES])
        past = sb("past", [1, NTILES, E])
        pastw = sb("pastw", [1, NTILES, E])
        te = sb("te", [1, NTILES])
        tep = sb("tep", [1, 4 * WORDS + 2])
        tw = sb("tw", [1, NTILES])
        ta = sb("ta", [1, NTILES])
        tb = sb("tb", [1, NTILES])
        packf = sb("packf", [1, WORDS])
        tab_e = sb("tab_e", [1, WORDS], I32)
        tab_row = sb("tab_row", [1, NTILES], I32)

        raw = w1_raw[:, :, :].rearrange("p e f -> p (e f)")

        def carve(start, n, width):
            return raw[:, start:start + n * width].rearrange("p (n w) -> p n w", n=n)

        xr = carve(0, 4, ROW)
        xrT = carve(4 * ROW, 2, P)
        hb = carve(4 * ROW + 2 * P, 2, F)
        hT = carve(4 * ROW + 2 * (P + F), 2, FC * P)
        yb = carve(4 * ROW + 2 * (P + 2 * F), 2, D)
        yw = carve(4 * ROW + 2 * (P + 2 * F + D), 4, D)
        yi = sb("yi", [P, 4], U32)
        yp = sb("yp", [P, 4])

        yin = w1T[:, 0:CB * CG * SLOTS * D].rearrange("p (u c d) -> p u c d", u=CB, c=CG)
        ysum = w2T[:, 0:CB * CG * D].rearrange("p (u c d) -> p u c d", u=CB, c=CG)

        s_const = sem("s_const")
        s_late = sem("s_late")
        s_waited = sem("s_waited")
        s_pc = sem("s_pc")
        s_w = sem("s_w")
        s_wl = sem("s_wl")
        s_b = sem("s_b")
        s_wt = sem("s_wt")
        s_wts = sem("s_wts")
        s_dc = sem("s_dc")
        s_xin = [sem(f"s_xin{p}") for p in range(2)]
        s_adjin = [sem(f"s_adjin{p}") for p in range(2)]
        s_store = [sem(f"s_store{p}") for p in range(2)]
        s_pack = [sem(f"s_pack{p}") for p in range(2)]
        s_ln = sem("s_ln")
        s_rstd = sem("s_rstd")
        s_xn = sem("s_xn")
        s_xb = sem("s_xb")
        s_xTp = sem("s_xTp")
        s_xT = sem("s_xT")
        s_qkp = sem("s_qkp")
        s_qf = sem("s_qf")
        s_qk = sem("s_qk")
        s_parts = sem("s_parts")
        s_vp = sem("s_vp")
        s_v = sem("s_v")
        s_ap = sem("s_ap")
        s_a = sem("s_a")
        s_s = sem("s_s")
        s_max = sem("s_max")
        s_exp = sem("s_exp")
        s_t = sem("s_t")
        s_mul = sem("s_mul")
        s_av = sem("s_av")
        s_o = sem("s_o")
        s_otp = sem("s_otp")
        s_on = sem("s_on")
        s_ontp = sem("s_ontp")
        s_ont = sem("s_ont")
        s_y = sem("s_y")
        s_res = sem("s_res")
        s_ln2 = sem("s_ln2")
        s_rstd2 = sem("s_rstd2")
        s_x2 = sem("s_x2")
        s_x2c = sem("s_x2c")
        s_x2tp = sem("s_x2tp")
        s_x2t = sem("s_x2t")
        s_gate = sem("s_gate")
        s_top = sem("s_top")
        s_gexp = sem("s_gexp")
        s_rank = sem("s_rank")
        s_gin = sem("s_gin")
        s_rin = sem("s_rin")
        s_pos = sem("s_pos")
        s_sc = [sem(f"s_sc{p}") for p in range(2)]
        s_pad = sem("s_pad")
        s_padd = sem("s_padd")
        s_sur = sem("s_sur")
        s_tab = sem("s_tab")
        s_w1 = sem("s_w1")
        s_w2 = sem("s_w2")
        s_wp = sem("s_wp")
        f_in = [sem(f"f_in{p}") for p in range(4)]
        f_meta = sem("f_meta")
        f_xp = sem("f_xp")
        f_xT = sem("f_xT")
        f_h = sem("f_h")
        f_hb = sem("f_hb")
        f_hp = sem("f_hp")
        f_hT = sem("f_hT")
        f_y = sem("f_y")
        f_yw = sem("f_yw")
        f_sc = [sem(f"f_sc{p}") for p in range(4)]
        c_in = [sem(f"c_in{p}") for p in range(CB)]
        c_sum = sem("c_sum")
        c_out = sem("c_out")

        block = ctx.enter_context(nc.Block())

        def ge_apart(eng, s, v):
            wait_apart(eng, s_waited, s, v)

        def group_of(m):
            return m // (GR // NC), 2 * (m % (GR // NC))

        EARLY = GR // 2

        def expert_of(b, m):
            return m // 2 if isinstance(b, int) and b == NB and m % 2 else None

        def has(v, off, count):
            return not isinstance(v, int) or 0 <= v + off < count

        def ge(eng, s, v):
            if not isinstance(v, int) or v > 0:
                eng.wait_ge(s, v)

        def pipeline(eng, body, lo, first, times, step, hi, chains=()):
            for v in range(lo, first):
                body(v, v // step, v % step)
            with eng.Fori(0, times) as it:
                for chain, per in chains:
                    chain.enter(it, per)
                i = it + first // step
                for u in range(step):
                    body(it * step + (first + u), i, u)
            for chain, _ in chains:
                chain.leave(times)
            for v in range(first + step * times, hi):
                body(v, v // step, v % step)

        def batches(eng, body, chains=()):
            pipeline(eng, body, -4, 4, (NB - 8) // 2, 2, NB + 3, chains)

        def tiles(eng, body, chains=()):
            pipeline(eng, body, -2, 4, NTILES // 4 - 2, 4, NTILES + 1, chains)

        def use(i, par, off):
            return i + (par + off) // 2, (par + off) % 2

        def batch_of(view, b):
            return view[b] if isinstance(b, int) else view[ds(b, 1)].rearrange("o p c d -> (o p) c d")

        def tile_span(t, n):
            return slice(t * D, (t + n) * D) if isinstance(t, int) else ds(t * D, n * D)

        def padding(eng, experts):
            eng.wait_ge(s_pad, 1)
            for e in experts:
                end = eng.value_load(end_row[0:1, e:e + 1], min_val=e * CAP, max_val=e * CAP + T)
                eng.dma_start(xs[ds(end, P)], padrow[:, e, :]).then_inc(s_padd, DMA)

        def halves(tile):
            return tile[:, :].rearrange("p (k t) -> p k t", k=2)

        def part_of(q, s):
            return parts[:, q, s:2 * PARTS - s:2 * PARTS - 1 - 2 * s, :]

        def chunks(ap):
            return ap.rearrange("p (c d) -> p c d", c=NC)

        @block.sync
        def _(sp):
            def small_weights():
                for k, w in enumerate((Wq, Wk, Wv, Wo)):
                    sp.dma_start(w_raw[:, k, :], w).then_inc(s_w, DMA)
                sp.dma_start(wg_raw[:, :], Wg).then_inc(s_w, DMA)
                sp.dma_start(bo_bc[:, :], bo.unsqueeze(0).broadcast_to([P, D])).then_inc(s_w, DMA)
                sp.dma_start(bg_bc[:, :], bg.unsqueeze(0).broadcast_to([P, E])).then_inc(s_w, DMA)

            def body(b, i, par):
                if has(b, 4, NB):
                    _, q = use(i, par, 4)
                    ge_apart(sp, s_xn, b + 3)
                    ge(sp, s_xb, b + 3)
                    sp.dma_start(chunks(xin[:, q, :]), batch_of(x_v, b + 4)).then_inc(s_xin[q], DMA)
                if isinstance(b, int) and b == -4:
                    small_weights()
                if has(b, 2, NB):
                    h, q = use(i, par, 2)
                    ge_apart(sp, s_ap, b + 1)
                    sp.dma_start(chunks(adj_in[:, q, :]), batch_of(adj_v, b + 2)).then_inc(s_adjin[q], DMA)
                    ge_apart(sp, s_parts, b + 3)
                    ge(sp, s_pack[q], DMA * 2 * len(PRODUCTS) * h)
                    sp.dma_start(parts_dram[q].rearrange("s p t -> p s t"), parts[:, q, :, :]).then_inc(s_store[q], DMA)
                    ge_apart(sp, s_store[q], DMA * (h + 1))
                    ge_apart(sp, s_s, GR * (b + 1))
                    src = parts_dram[q].rearrange("s (d h) t -> (s d) h t", h=HEADS)
                    row = 0
                    for n in PRODUCTS:
                        rows_n = slice(row, row + n * HD)
                        row += n * HD
                        for dst, at in ((qp, 0), (kp, 2 * PARTS - n)):
                            sp.dma_start(dst[rows_n, q], src[at * HD:(at + n) * HD]).then_inc(s_pack[q], DMA)
                if isinstance(b, int) and b in loads:
                    e = loads.index(b)
                    sp.dma_start(w1_raw[:, e, :].rearrange("p (c d) -> p c d", c=FC),
                                 W1[e].rearrange("(c p) d -> p c d", p=P)).then_inc(s_wl, DMA)
                    sp.dma_start(w2_raw[:, e, :], W2[e]).then_inc(s_wl, DMA)
                    sp.dma_start(b1_bc[:, e * F:(e + 1) * F], b1[e:e + 1].broadcast_to([P, F])).then_inc(s_b, DMA)
                    sp.dma_start(b2_bc[:, e * D:(e + 1) * D], b2[e:e + 1].broadcast_to([P, D])).then_inc(s_b, DMA)

            loads = (-1, 0, 1, 2, 3, NB - 4, NB - 3, NB - 2)
            batches(sp, body)

            padding(sp, range(0, E, 2))

            sp.wait_ge(s_tab, 1)
            sp.wait_ge(s_wp, 2 * E)
            sp.wait_ge(s_padd, DMA * E)
            sp.wait_ge(s_sur, DMA)
            for p in range(2):
                sp.wait_ge(s_sc[p], DMA * NC * SLOTS * (NB // 2))

            def body(t, i, u):
                if has(t, 0, NTILES):
                    first_row = sp.value_load(tab_row[0:1, t:t + 1] if isinstance(t, int) else tab_row[0:1, ds(t, 1)],
                                              min_val=0, max_val=E * CAP + (SURPLUS - 1) * P)
                    ge(sp, f_xp, t - 3)
                    ge_apart(sp, f_meta, t - 3)
                    sp.dma_start(xr[:, u, :], xs[ds(first_row, P)]).then_inc(f_in[u], DMA)

            tiles(sp, body)

            for p in range(4):
                sp.wait_ge(f_sc[p], DMA * (NTILES // 4))
            ys_v = ys[0:SLOTS * T].rearrange("(g c p s) d -> g p c (s d)", c=CG, p=P, s=SLOTS)

            def body(g, i, u):
                ge_apart(sp, c_sum, g - (CB - 1))
                sp.dma_start(yin[:, u], ys_v[g] if isinstance(g, int) else
                             ys_v[ds(g, 1)].rearrange("o p c d -> (o p) c d")).then_inc(c_in[u], DMA)

            pipeline(sp, body, 0, CB, NT // CG // CB - 1, CB, NT // CG)

        @block.gpsimd
        def _(pool):
            g = nc.gpsimd
            link = Chain(pool, s_pc, s_waited)
            link(g.memset(ident[:, :], 1.0))
            link(g.affine_select(out=ident[:, :], in_=ident[:, :], compare_op=ALU.is_equal, fill=0.0,
                                 base=0, pattern=[[-1, P]], channel_multiplier=1))
            link.count(g.memset(neg_half[:, :], -0.5))
            link.count(g.memset(minus1[:, :], -1.0))
            link(g.memset(adj_eps[:, :], ADJ_EPS))
            pool.sem_inc(s_const, 1)

            def later_constants():
                link.count(g.memset(before[:, :], 1.0))
                link.count(g.memset(padrow[:, :, :], 0.0))
                link.count(g.memset(ones_bf[:, :], 1.0))
                link(g.memset(vaug[:, :, :, :, :], 1.0))
                link.count(g.affine_select(out=before[:, :], in_=before[:, :], compare_op=ALU.is_gt, fill=0.0,
                                           base=0, pattern=[[1, P]], channel_multiplier=-1))
                link.count(g.iota(padrow[:, :, D:D + 1].rearrange("p e o -> p (e o)"), pattern=[[P, PADS]],
                                  base=SLOTS * T, channel_multiplier=1, allow_small_or_imprecise_dtypes=True))
                for tile, step, n in ((iota_e, 1, E), (base, CAP, E), (ebase, CAP, E), (iota_t, 1, NTILES)):
                    link.count(g.iota(tile[:, :], pattern=[[step, n]], base=0, channel_multiplier=0,
                                      allow_small_or_imprecise_dtypes=True))
                for par in range(2):
                    link.count(g.iota(rows[:, par, :, :, D], pattern=[[SLOTS * P, NC], [1, SLOTS]],
                                      base=(par - 2) * SLOTS * N, channel_multiplier=SLOTS,
                                      allow_small_or_imprecise_dtypes=True))
                link.after()
                pool.sem_inc(s_late, 1)
                pool.dma_start(xs[E * CAP:E * CAP + SURPLUS * P].rearrange("(k p) r -> p k r", p=P),
                               padrow[:, E:PADS, :]).then_inc(s_sur, DMA)

            def body(b, i, par):
                if has(b, -3, NB):
                    h, q = use(i, par, -3)
                    ge_apart(pool, s_sc[q], DMA * NC * SLOTS * h)
                    link(g.tensor_scalar(rows[:, q, :, :, D], rows[:, q, :, :, D], float(2 * SLOTS * N), None, ALU.add))
                    ge_apart(pool, s_pos, b - 2)
                    for c in range(NC):
                        for s in range(SLOTS):
                            k = c * SLOTS + s
                            g.indirect_dma_start(xs, bass.IndirectOffsetOnAxis(ap=posi[:, q, k:k + 1], axis=0),
                                                 rows[:, q, c, s, :], None).then_inc(s_sc[q], DMA)
                if has(b, 3, NB):
                    h, q = use(i, par, 3)
                    ge_apart(pool, s_ln, b + 4)
                    link(g.tensor_scalar(var_e[:, :], mv[:, q, :, 1], LN_EPS, None, ALU.add))
                    link(g.tensor_tensor(rstd[:, q, :], var_e[:, :], neg_half[:, :], ALU.pow))
                    link(g.tensor_tensor(shift[:, q, :], mv[:, q, :, 0], rstd[:, q, :], ALU.mult))
                    g.tensor_tensor(shift[:, q, :], shift[:, q, :], minus1[:, :], ALU.mult).then_inc(s_rstd, 1)
                    if isinstance(b, int) and b == -3:
                        pool.wait_ge(s_w, DMA * 7)
                    pool.wait_ge(s_xin[q], DMA * (h + 1))
                    g.tensor_tensor(chunks(x1[:, tile_span((b + 3) * NC, NC)]), chunks(xin[:, q, :]),
                                    bo_bc[:, :].unsqueeze(1).broadcast_to([P, NC, D]), ALU.add).then_inc(s_xb, 1)
                if isinstance(b, int) and b == -1:
                    later_constants()
                if has(b, 2, NB):
                    h, q = use(i, par, 2)
                    pool.wait_ge(s_qk, b + 3)
                    link.count(g.tensor_tensor(halves(rest), halves(qk), part_of(q, 0), ALU.subtract))
                    link(g.tensor_tensor(part_of(q, 1), halves(qk), part_of(q, 0), ALU.subtract))
                    g.tensor_tensor(part_of(q, 2), halves(rest), part_of(q, 1),
                                    ALU.subtract).then_inc(s_parts, 1)
                if has(b, -1, NB):
                    ge_apart(pool, s_ln2, b)
                    ge_apart(pool, s_x2, b - 1)
                    link(g.tensor_scalar(var2[:, :], mv2[:, :, 1], LN_EPS, None, ALU.add))
                    link(g.tensor_tensor(rstd2[:, :], var2[:, :], neg_half[:, :], ALU.pow))
                    link(g.tensor_tensor(shift2[:, :], mv2[:, :, 0], rstd2[:, :], ALU.mult))
                    g.tensor_tensor(shift2[:, :], shift2[:, :], minus1[:, :], ALU.mult).then_inc(s_rstd2, 1)

            batches(pool, body, [(link, 2 * 9)])
            def body(t, i, u):
                if has(t, -1, NTILES):
                    v = (u - 1) % 4
                    ge_apart(pool, f_yw, t)
                    g.indirect_dma_start(ys, bass.IndirectOffsetOnAxis(ap=yi[:, v:v + 1], axis=0),
                                         yw[:, v, :], None).then_inc(f_sc[v], DMA)

            tiles(pool, body)

        @block.scalar
        def _(act):
            s = nc.scalar
            act.wait_ge(s_const, 1)
            s.activation(warm[:, :], adj_eps[:, :], ACT.Exp).then_inc(s_waited, 1)

            def exps(b, m, G):
                act.wait_ge(s_max, G + 1)
                ge(act, s_t, G - 1)
                for j in range(2):
                    ins = s.activation(ex[:, m % 2, j * N:(j + 1) * N], psS[:, m % 2, j * N:(j + 1) * N],
                                       ACT.Exp, bias=nmax[:, m % 4, j:j + 1])
                ins.then_inc(s_exp, 1)

            def body(b, i, par):
                for m in range(GR):
                    if m == 0 and has(b, -1, NB):
                        act.wait_ge(s_av, GR * b)
                        s.activation(o_sb[:, :], psO[:, :], ACT.Copy).then_inc(s_o, 1)
                    if m + 2 < GR and has(b, 0, NB) or m + 2 >= GR and has(b, 1, NB):
                        exps(b, (m + 2) % GR, b * GR + (m + 2))
                    if m == 0 and has(b, 2, NB):
                        _, q = use(i, par, 2)
                        act.wait_ge(s_xTp, b + 3)
                        s.activation(xT[:, q, :], psX[:, 0:N], ACT.Copy).then_inc(s_xT, 1)
                    if m == 1 and has(b, -2, NB):
                        h, q = use(i, par, -2)
                        ge(act, s_sc[q], DMA * NC * SLOTS * h)
                        ge_apart(act, s_rstd2, b - 1)
                        for c in range(NC):
                            ins = s.activation(rows[:, q, c, 0, 0:D], x1[:, tile_span((b - 2) * NC + c, 1)],
                                               ACT.Identity, bias=shift2[:, c:c + 1], scale=rstd2[:, c:c + 1])
                        ins.then_inc(s_x2, 1)
                    if m == 1 and has(b, 2, NB):
                        act.wait_ge(s_qkp, b + 3)
                        ge(act, s_parts, b + 2)
                        s.activation(qk[:, :], psQ[:, :], ACT.Copy).then_inc(s_qf, 1)
                    if m == 2 and has(b, -2, NB):
                        act.wait_ge(s_x2tp, b - 1)
                        s.activation(x2T[:, :], psX[:, 0:N], ACT.Copy).then_inc(s_x2t, 1)
                    if m == 2 and has(b, 2, NB):
                        h, q = use(i, par, 2)
                        ge(act, s_store[q], DMA * h)
                        s.activation(part_of(q, 0), halves(psQ), ACT.Copy).then_inc(s_qk, 1)
                    if m == 3 and has(b, -1, NB):
                        act.wait_ge(s_ontp, b)
                        s.activation(onT[:, :], psR[:, 0:N], ACT.Copy).then_inc(s_ont, 1)
                    if m == 4 and has(b, -2, NB):
                        _, q = use(i, par, -2)
                        act.wait_ge(s_x2, b - 1)
                        s.activation(rows[:, q, :, 1, 0:D], rows[:, q, :, 0, 0:D], ACT.Copy).then_inc(s_x2c, 1)
                    if m == 5 and has(b, -1, NB):
                        ge_apart(act, s_y, b)
                        s.activation(x1[:, tile_span((b - 1) * NC, NC)], psR[:, N:2 * N], ACT.Copy).then_inc(s_res, 1)
                    if m == 5 and has(b, 3, NB):
                        _, q = use(i, par, 3)
                        act.wait_ge(s_rstd, b + 4)
                        ge(act, s_xTp, b + 2)
                        for c in range(NC):
                            ins = s.activation(xn[:, q, c * D:(c + 1) * D], xin[:, q, c * D:(c + 1) * D], ACT.Identity,
                                               bias=shift[:, q, c:c + 1], scale=rstd[:, q, c:c + 1])
                        ins.then_inc(s_xn, 1)
                    if m == 6 and has(b, -2, NB):
                        act.wait_ge(s_top, b - 1)
                        for c in range(NC):
                            ins = s.activation(egap[:, c:c + 1], top[:, c, 0:1], ACT.Exp,
                                               bias=top[:, c, 1:2], scale=-1.0)
                        ins.then_inc(s_gexp, 1)
                    if m == 6 and has(b, 1, NB):
                        _, q = use(i, par, 1)
                        act.wait_ge(s_ap, b + 2)
                        ge(act, s_mul, GR * b)
                        s.activation(adjT[:, q, :, :], psQ[:, :].rearrange("p (c k) -> p c k", c=NC),
                                     ACT.Identity, bias=adj_eps[:, 0:1]).then_inc(s_a, 1)
                    if m == 7 and has(b, 1, NB):
                        _, q = use(i, par, 1)
                        if isinstance(b, int) and b == -1:
                            act.wait_ge(s_late, 1)
                        act.wait_ge(s_vp, b + 2)
                        ge(act, s_av, GR * b)
                        s.activation(vaug[:, q, :, :, 0:HD],
                                     psX[:, 0:N].rearrange("p (c h d) -> p c h d", c=NC, h=HEADS),
                                     ACT.Copy).then_inc(s_v, 1)
                    e = expert_of(b, m)
                    if e is not None:
                        act.wait_ge(s_wp, 2 * e + 2)
                        s.activation(w2T[:, e * FC * D:(e + 1) * FC * D], psT[:, e % 2, :], ACT.Copy).then_inc(s_w2, 1)

            batches(act, body)
            padding(act, range(1, E, 2))
            for e in range(EARLY, E):
                act.wait_ge(s_wp, 2 * e + 1)
                s.activation(w1T[:, e * F:(e + 1) * F], psS[:, e % 2, :], ACT.Copy).then_inc(s_w1, 1)
                act.wait_ge(s_wp, 2 * e + 2)
                s.activation(w2T[:, e * FC * D:(e + 1) * FC * D], psT[:, e % 2, :], ACT.Copy).then_inc(s_w2, 1)

            def body(t, i, u):
                if has(t, 2, NTILES):
                    act.wait_ge(f_xp, t + 3)
                    ge(act, f_h, t + 1)
                    s.activation(xrT[:, u % 2, :], (psX, psO)[u % 2][:, 0:P], ACT.Copy).then_inc(f_xT, 1)
                if has(t, 0, NTILES):
                    act.wait_ge(f_hp, t + 1)
                    ge(act, f_y, t - 1)
                    s.activation(hT[:, u % 2, :], psT[:, u % 2, :], ACT.Relu).then_inc(f_hT, 1)

            tiles(act, body)

            def body(g, i, u):
                act.wait_ge(c_sum, g + 1)
                src = x1[:, tile_span(g * CG, CG)].rearrange("p (c d) -> p c d", c=CG)
                dst = out_v[:, g * CG:(g + 1) * CG, :] if isinstance(g, int) else out_v[:, ds(g * CG, CG), :]
                act.dma_start(dst, src).then_inc(c_out, DMA)

            pipeline(act, body, 0, CB, NT // CG // CB - 1, CB, NT // CG)
            act.wait_ge(c_out, DMA * (NT // CG))

        @block.vector
        def _(dve):
            v = nc.vector
            link = Chain(dve, s_dc, s_waited)
            def by_depth(k):
                return wT[:, k, :].rearrange("p (d h) -> p h d", h=HEADS), \
                    psS[:, 0, k * P:(k + 1) * P].rearrange("p (h d) -> p h d", h=HEADS)

            def small_weights():
                dve.wait_ge(s_wt, 1)
                v.tensor_scalar(*by_depth(0), float(HD) ** -0.5, None, ALU.mult).then_inc(s_wts, 1)
                v.tensor_copy(*by_depth(1)).then_inc(s_wts, 1)
                v.tensor_copy(wT[:, 2:4, :].rearrange("p k o -> p (k o)"), psS[:, 0, 2 * P:4 * P]).then_inc(s_wts, 1)
                v.tensor_copy(wgT[:, :], psX[:, 0:E]).then_inc(s_wts, 1)
                dve.wait_ge(s_w, DMA * 7)

            def body(b, i, par):
                for m in range(GR):
                    end, last, tail, front = has(b, -3, NB), has(b, -2, NB), has(b, -1, NB), has(b, 3, NB)
                    _, qe = use(i, par, -3)
                    _, q2 = use(i, par, -2)
                    h3, q3 = use(i, par, 3)
                    G = b * GR + m
                    if m + 2 < GR and has(b, 0, NB) or m + 2 >= GR and has(b, 1, NB):
                        dve.wait_ge(s_s, G + 3)
                        v.tensor_reduce(nmax[:, (m + 2) % 4, :], psS[:, m % 2, :].rearrange("p (j k) -> p j k", j=2),
                                        AX.X, ALU.max, negate=True).then_inc(s_max, 1)

                    if m == 0 and end:
                        link.after()
                        link.count(v.tensor_reduce(posf[:, :, :], possel[:, :, :, :], AX.X, ALU.add))
                        link.count(v.tensor_tensor(rows[:, qe, :, 1, D + 1:D + 2], rows[:, qe, :, 0, D + 1:D + 2],
                                                   egap[:, :].unsqueeze(2), ALU.mult))
                    if m == 3 and tail:
                        link.after()
                        v.tensor_tensor(on[:, :].rearrange("p (k d) -> p k d", d=HD),
                                        psR[:, :].rearrange("p (k w) -> p k w", w=VW)[:, :, 0:HD],
                                        rec[:, :].unsqueeze(2).broadcast_to([P, 16, HD]), ALU.mult).then_inc(s_on, 1)
                    if m == 4 and last:
                        ge_apart(dve, s_gin, b - 1)
                        for c in range(NC):
                            link.count(v.max(top[:, c, :], gate[:, c, :]))
                    if m == 6 and tail:
                        ge_apart(dve, s_res, b)
                        for c in range(NC):
                            link.count(v.bn_stats(stats2[:, c, :], x1[:, tile_span((b - 1) * NC + c, 1)]))
                    if m == 7 and last:
                        link.after()
                        v.tensor_tensor(base[:, :], psR[:, NC * E:(NC + 1) * E], base[:, :], ALU.add).then_inc(s_rin, 1)
                        dve.wait_ge(s_gexp, b - 1)
                        link.count(v.tensor_scalar(den2[:, :], egap[:, :], 1.0, None, ALU.add))

                    if has(b, 0, NB):
                        qc, _ = group_of(m)
                        if m == 0:
                            dve.wait_ge(s_a, b + 1)
                        dve.wait_ge(s_t, G + 1)
                        ge(dve, s_av, G - 1)
                        v.tensor_tensor(pT[:, m % 2, :].rearrange("p (j c q) -> p j c q", j=2, c=NC),
                                        psT[:, m % 2, :].rearrange("p (j c q) -> p j c q", j=2, c=NC),
                                        adjT[:, par, :, qc * P:(qc + 1) * P].unsqueeze(1)
                                        .broadcast_to([P, 2, NC, P]), ALU.mult).then_inc(s_mul, 1)

                    if m == 0 and end:
                        link.after()
                        dve.wait_ge(s_x2c, b - 2)
                        v.tensor_copy(posi[:, qe, :], posf[:, :, :].rearrange("p c s -> p (c s)")).then_inc(s_pos, 1)
                    if m == 1 and front:
                        ge_apart(dve, s_ln, b + 3)
                        ge_apart(dve, s_xin[q3], DMA * (h3 + 1))
                        for c in range(NC):
                            link.count(v.bn_stats(stats[:, c, :], xin[:, q3, c * D:(c + 1) * D]))
                    if m == 3 and last:
                        dve.wait_ge(s_gate, b - 1)
                        v.tensor_tensor(gate[:, :, :], psX[:, 0:NC * E].rearrange("p (c e) -> p c e", c=NC),
                                        bg_bc[:, :].unsqueeze(1).broadcast_to([P, NC, E]), ALU.add).then_inc(s_gin, 1)
                    if m == 2 and tail:
                        dve.wait_ge(s_otp, b)
                        link.count(v.reciprocal(rec[:, :].unsqueeze(2),
                                                psR[:, :].rearrange("p (k w) -> p k w", w=VW)[:, :, HD:HD + 1]))
                    if m == 3 and front:
                        link.after_apart()
                        for c in range(NC):
                            ins = v.bn_aggr(mv[:, q3, c, :], stats[:, c, :])
                            if c < NC - 1:
                                link.count(ins)
                        ins.then_inc(s_ln, 1)
                    if m == 4 and last:
                        link.after_apart()
                        for c in range(NC):
                            link.count(v.max_index(topi[:, c, :], top[:, c, :], gate[:, c, :]))
                    if m == 5 and last:
                        link.after()
                        v.tensor_tensor(
                            onehot[:, :, :, :], iota_e[:, :].unsqueeze(1).unsqueeze(1).broadcast_to([P, NC, SLOTS, E]),
                            topi[:, :, 0:SLOTS].unsqueeze(3).broadcast_to([P, NC, SLOTS, E]),
                            ALU.is_equal).then_inc(s_top, 1)
                    if m == 6 and tail:
                        link.after_apart()
                        for c in range(NC):
                            ins = v.bn_aggr(mv2[:, c, :], stats2[:, c, :])
                            if c < NC - 1:
                                link.count(ins)
                        ins.then_inc(s_ln2, 1)
                    if m == 6 and last:
                        dve.wait_ge(s_rank, b - 1)
                        ge(dve, s_rin, b - 2)
                        link.count(v.tensor_tensor(posn[:, :, :], psR[:, 0:NC * E].rearrange("p (c e) -> p c e", c=NC),
                                                   base[:, :].unsqueeze(1).broadcast_to([P, NC, E]), ALU.add))
                    if m == 7 and last:
                        link.after()
                        ge(dve, s_top, b - 1)
                        link.count(v.tensor_tensor(possel[:, :, :, :], onehot[:, :, :, :],
                                                   posn[:, :, :].unsqueeze(2).broadcast_to([P, NC, SLOTS, E]),
                                                   ALU.mult))
                        link.count(v.reciprocal(rows[:, q2, :, 0, D + 1:D + 2], den2[:, :].unsqueeze(2)))
                    if isinstance(b, int) and b == -3 and m == GR - 1:
                        small_weights()
                    if isinstance(b, int) and b == 0 and m == 0:
                        dve.wait_ge(s_late, 1)
                    e = expert_of(b, m)
                    if e is not None:
                        dve.wait_ge(s_wp, 2 * e + 1)
                        v.tensor_copy(w1T[:, e * F:(e + 1) * F], psS[:, e % 2, :]).then_inc(s_w1, 1)

            batches(dve, body, [(link, 2 * 17)])

            dve.wait_ge(s_rin, NB)
            v.tensor_copy(end_row[:, :], base[0:1, :]).then_inc(s_pad, 1)
            link(v.tensor_tensor(ntile[:, :], base[:, :], ebase[:, :], ALU.subtract))
            link(v.tensor_scalar(cnt_i[:, :], ntile[:, :], float(P - 1), None, ALU.add))
            link(v.tensor_scalar(cnt_t[:, :], cnt_i[:, :], 7, None, ALU.arith_shift_right))
            link(v.tensor_copy(ntile[:, :], cnt_t[:, :]))
            link(v.tensor_copy(endt[:, :], ntile[:, :]))
            for e in range(1, E):
                link(v.tensor_tensor(endt[:, e:e + 1], endt[:, e:e + 1], endt[:, e - 1:e], ALU.add))
            link(v.tensor_tensor(past[:, :, :], iota_t[:, :].unsqueeze(2).broadcast_to([1, NTILES, E]),
                                 endt[0:1, :].unsqueeze(1).broadcast_to([1, NTILES, E]), ALU.is_ge))
            link(v.tensor_reduce(te[:, :], past[:, :, :], AX.X, ALU.add))
            link(v.tensor_tensor(pastw[:, :, :], past[:, :, :],
                                 ntile[0:1, :].unsqueeze(1).broadcast_to([1, NTILES, E]), ALU.mult))
            link(v.tensor_reduce(tw[:, :], pastw[:, :, :], AX.X, ALU.add))
            link(v.tensor_tensor(ta[:, :], iota_t[:, :], tw[:, :], ALU.subtract))
            link(v.memset(tep[:, :], 0.0))
            link(v.tensor_scalar(tep[:, 5:NTILES + 5], te[:, :], float(E - 1), None, ALU.min))
            link(v.memset(packf[:, :], 0.0))
            for k in range(6):
                link(v.scalar_tensor_tensor(out=packf[:, :], in0=tep[:, k:k + 4 * WORDS - 3:4], scalar=float(E ** k),
                                            in1=packf[:, :], op0=ALU.mult, op1=ALU.add))
            link(v.tensor_copy(tab_e[:, :], packf[:, :]))
            link(v.tensor_scalar(tb[:, :], te[:, :], float(CAP), None, ALU.mult))
            v.scalar_tensor_tensor(out=tab_row[:, :], in0=ta[:, :], scalar=float(P), in1=tb[:, :],
                                   op0=ALU.mult, op1=ALU.add).then_inc(s_tab, 1)

            dve.wait_ge(s_b, DMA * 2 * E)
            dve.wait_ge(s_tab, 1)

            expert = Experts(dve, tab_e)

            def body(t, i, u):
                if u == 0 or isinstance(t, int) and t == -2:
                    expert.take()
                if has(t, 1, NTILES):
                    w = (u + 1) % 2
                    e = expert(u, 1)
                    dve.wait_ge(f_h, t + 2)
                    ge(dve, f_hp, t)
                    v.tensor_tensor(hb[:, w, :], psS[:, w, :], b1_bc[:, ds(e * F, F)], ALU.add).then_inc(f_hb, 1)
                if u == 3 and has(t, 1, NTILES + 1):
                    expert.load_next(i)
                if has(t, 1, NTILES):
                    r, n = (u + 1) % 4, i + (u + 1) // 4
                    dve.wait_ge(f_in[r], DMA * (n + 1))
                    ge(dve, f_sc[r], DMA * n)
                    link.count(v.tensor_copy(yi[:, r:r + 1], xr[:, r, D:D + 1]))
                    v.tensor_copy(yp[:, r:r + 1], xr[:, r, D + 1:D + 2]).then_inc(f_meta, 1)
                if has(t, -1, NTILES):
                    w, r = (u - 1) % 2, (u - 1) % 4
                    e = expert(u, -1)
                    dve.wait_ge(f_y, t)
                    ps = psQ if w == 0 else psR
                    link(v.tensor_tensor(yb[:, w, :], ps[:, 0:D], b2_bc[:, ds(e * D, D)], ALU.add))
                    v.tensor_scalar(yw[:, r, :], yb[:, w, :], yp[:, r:r + 1], None,
                                    ALU.mult).then_inc(f_yw, 1)

            tiles(dve, body, [(link, 8)])

            def body(g, i, u):
                dve.wait_ge(c_in[u], DMA * (i + 1))
                link(v.tensor_tensor(ysum[:, u], yin[:, u, :, 0:D], yin[:, u, :, D:2 * D], ALU.add))
                r = x1[:, tile_span(g * CG, CG)]
                v.tensor_tensor(r, ysum[:, u].rearrange("p c d -> p (c d)"), r, ALU.add).then_inc(c_sum, 1)

            pipeline(dve, body, 0, CB, NT // CG // CB - 1, CB, NT // CG, [(link, CB)])

        @block.tensor
        def _(pe):
            t_ = nc.tensor
            pe.wait_ge(s_w, DMA * 7)
            pe.wait_ge(s_const, 1)
            for k in range(4):
                t_.transpose(psS[:, 0, k * P:(k + 1) * P], w_raw[:, k, :], ident[:, :])
            t_.transpose(psX[:, 0:E], wg_raw[:, :], ident[0:E, 0:E]).then_inc(s_wt, 1)
            pe.wait_ge(s_wts, 4)

            def scores(b, i, par, off, m, G):
                h, q = use(i, par, off)
                if m == 0:
                    pe.wait_ge(s_pack[q], DMA * 2 * len(PRODUCTS) * (h + 1))
                ge(pe, s_exp, G - 1)
                qc, h0 = group_of(m)
                for j in range(2):
                    ins = t_.matmul(psS[:, m % 2, j * N:(j + 1) * N], qp[:, q, h0 + j, qc * P:(qc + 1) * P],
                                    kp[:, q, h0 + j, :], start=True, stop=True)
                ins.then_inc(s_s, 1)

            def transposes(b, m):
                G = b * GR + m
                pe.wait_ge(s_exp, G + 1)
                ge(pe, s_mul, G - 1)
                for k in range(4):
                    ins = t_.transpose(psT[:, m % 2, k * P:(k + 1) * P], ex[:, m % 2, k * P:(k + 1) * P], ident[:, :])
                ins.then_inc(s_t, 1)

            def values(b, q, m, G):
                if m == 0:
                    pe.wait_ge(s_v, b + 1)
                    ge(pe, s_o, b)
                pe.wait_ge(s_mul, G + 1)
                qc, h0 = group_of(m)
                col = (qc * (HEADS // HG) + h0 // HG) * P
                for j in range(2):
                    r = VW * ((h0 + j) % HG)
                    for c in range(NC):
                        ins = t_.matmul(psO[r:r + VW, col:col + P], vaug[:, q, c, h0 + j, :],
                                        pT[:, m % 2, (j * NC + c) * P:(j * NC + c + 1) * P],
                                        start=(c == 0), stop=(c == NC - 1))
                ins.then_inc(s_av, 1)

            def expert_matrices(e):
                pe.wait_ge(s_wl, DMA * 2 * E)
                ge(pe, s_w1, e - 1)
                for c in range(FC):
                    ins = t_.transpose(psS[:, e % 2, c * P:(c + 1) * P], w1_raw[:, e, c * D:(c + 1) * D], ident[:, :])
                ins.then_inc(s_wp, 1)
                ge(pe, s_w2, e - 1)
                for c in range(FC):
                    ins = t_.transpose(psT[:, e % 2, c * P:(c + 1) * P], w2_raw[:, e, c * P:(c + 1) * P], ident[:, :])
                ins.then_inc(s_wp, 1)

            def body(b, i, par):
                for m in range(GR):
                    if isinstance(b, int) and b == 0 and m == 0:
                        pe.wait_ge(s_late, 1)
                    if m + 2 < GR and has(b, 0, NB):
                        scores(b, i, par, 0, m + 2, b * GR + (m + 2))
                    if m + 2 >= GR and has(b, 1, NB):
                        scores(b, i, par, 1, m + 2 - GR, b * GR + (m + 2))
                    if has(b, 0, NB):
                        transposes(b, m)
                    if m == 0 and has(b, -1, NB):
                        values(b - 1, (par + 1) % 2, GR - 1, b * GR - 1)
                    if m > 0 and has(b, 0, NB):
                        values(b, par, m - 1, b * GR + (m - 1))
                    if m == 0 and has(b, 2, NB):
                        _, q = use(i, par, 2)
                        pe.wait_ge(s_xn, b + 3)
                        ge(pe, s_v, b + 1)
                        for c in range(NC):
                            ins = t_.transpose(psX[:, c * P:(c + 1) * P], xn[:, q, c * D:(c + 1) * D], ident[:, :])
                        ins.then_inc(s_xTp, 1)
                    if m == 1 and has(b, 2, NB):
                        _, q = use(i, par, 2)
                        pe.wait_ge(s_xT, b + 3)
                        ge(pe, s_a, b + 1)
                        for k in range(2):
                            ins = t_.matmul(psQ[:, k * N:(k + 1) * N], wT[:, k, :], xT[:, q, :], start=True, stop=True)
                        ins.then_inc(s_qkp, 1)
                    if m == 2 and has(b, -1, NB):
                        pe.wait_ge(s_o, b)
                        ge(pe, s_res, b - 1)
                        ge(pe, s_rin, b - 2)
                        for k in range(4):
                            ins = t_.transpose(psR[:, k * P:(k + 1) * P], o_sb[:, k * P:(k + 1) * P], ident[:, :])
                        ins.then_inc(s_otp, 1)
                    if m == 2 and has(b, -2, NB):
                        _, q = use(i, par, -2)
                        pe.wait_ge(s_x2, b - 1)
                        if has(b, 0, NB):
                            pe.wait_ge(s_v, b + 1)
                        for c in range(NC):
                            ins = t_.transpose(psX[:, c * P:(c + 1) * P], rows[:, q, c, 0, 0:D], ident[:, :])
                        ins.then_inc(s_x2tp, 1)
                    if m == 3 and has(b, -2, NB):
                        pe.wait_ge(s_x2t, b - 1)
                        for c in range(NC):
                            ins = t_.matmul(psX[:, c * E:(c + 1) * E], x2T[:, c * P:(c + 1) * P],
                                            wgT[:, :], start=True, stop=True)
                        ins.then_inc(s_gate, 1)
                    if m == 3 and has(b, -1, NB):
                        pe.wait_ge(s_on, b)
                        for c in range(NC):
                            ins = t_.transpose(psR[:, c * P:(c + 1) * P], on[:, c * D:(c + 1) * D], ident[:, :])
                        ins.then_inc(s_ontp, 1)
                    if 4 <= m < 4 + NC and has(b, -1, NB):
                        c = m - 4
                        if c == 0:
                            pe.wait_ge(s_ont, b)
                            pe.wait_ge(s_xb, b)
                        y = psR[:, N + c * P:N + (c + 1) * P]
                        t_.matmul(y, onT[:, c * P:(c + 1) * P], wT[:, 3, :], start=True, stop=False)
                        ins = t_.matmul(y, ident[:, :], x1[:, tile_span((b - 1) * NC + c, 1)],
                                        start=False, stop=True)
                        if c == NC - 1:
                            ins.then_inc(s_y, 1)
                    if m == 6 and has(b, 1, NB):
                        h, q = use(i, par, 1)
                        pe.wait_ge(s_adjin[q], DMA * (h + 1))
                        ge(pe, s_qk, b + 3 if has(b, 2, NB) else b + 2)
                        for c in range(NC):
                            for c0 in range(NC):
                                ins = t_.transpose(psQ[:, c * N + c0 * P:c * N + (c0 + 1) * P],
                                                   adj_in[:, q, c0 * N + c * P:c0 * N + (c + 1) * P], ident[:, :])
                        ins.then_inc(s_ap, 1)
                    if m == 6 and has(b, -2, NB):
                        pe.wait_ge(s_top, b - 1)
                        if has(b, -1, NB):
                            pe.wait_ge(s_res, b)
                        for c in range(NC):
                            for c0 in range(c + 1):
                                for k in range(SLOTS):
                                    t_.matmul(psR[:, c * E:(c + 1) * E], (before if c0 == c else ones_bf)[:, :],
                                              onehot[:, c0, k, :], start=(c0 == k == 0),
                                              stop=(c0 == c and k == SLOTS - 1))
                        for c in range(NC):
                            for k in range(SLOTS):
                                ins = t_.matmul(psR[:, NC * E:(NC + 1) * E], ones_bf[:, :], onehot[:, c, k, :],
                                                start=(c == k == 0), stop=(c == NC - 1 and k == SLOTS - 1))
                        ins.then_inc(s_rank, 1)
                    if m == 7 and has(b, 1, NB):
                        _, q = use(i, par, 1)
                        pe.wait_ge(s_xT, b + 3 if has(b, 2, NB) else b + 2)
                        ge(pe, s_gin, b - 1)
                        for c in range(NC):
                            ins = t_.matmul(psX[:, c * P:(c + 1) * P], xT[:, q, c * P:(c + 1) * P],
                                            wT[:, 2, :], start=True, stop=True)
                        ins.then_inc(s_vp, 1)
                    if expert_of(b, m) is not None:
                        expert_matrices(expert_of(b, m))

            batches(pe, body)
            for e in range(EARLY, E):
                expert_matrices(e)

            pe.wait_ge(s_w1, E)
            pe.wait_ge(s_w2, E)
            pe.wait_ge(s_tab, 1)

            expert = Experts(pe, tab_e)

            def body(t, i, u):
                if u == 0 or isinstance(t, int) and t == -2:
                    expert.take()
                if has(t, 2, NTILES):
                    w, r = u % 2, (u + 2) % 4
                    pe.wait_ge(f_in[r], DMA * (i + (u + 2) // 4 + 1))
                    ge(pe, f_xT, t + 1)
                    t_.transpose((psX, psO)[w][:, 0:P], xr[:, r, 0:D], ident[:, :]).then_inc(f_xp, 1)
                if has(t, 1, NTILES):
                    w = (u + 1) % 2
                    e = expert(u, 1)
                    pe.wait_ge(f_xT, t + 2)
                    ge(pe, f_hb, t)
                    t_.matmul(psS[:, w, :], xrT[:, w, :], w1T[:, ds(e * F, F)], start=True, stop=True).then_inc(f_h, 1)
                if u == 3 and has(t, 1, NTILES + 1):
                    expert.load_next(i)
                if has(t, 0, NTILES):
                    w = u % 2
                    pe.wait_ge(f_hb, t + 1)
                    ge(pe, f_hT, t - 1)
                    for c in range(FC):
                        ins = t_.transpose(psT[:, w, c * P:(c + 1) * P], hb[:, w, c * P:(c + 1) * P], ident[:, :])
                    ins.then_inc(f_hp, 1)
                if has(t, -1, NTILES):
                    w = (u - 1) % 2
                    e = expert(u, -1)
                    ps = psQ if w == 0 else psR
                    pe.wait_ge(f_hT, t)
                    ge(pe, f_yw, t - 2)
                    for c in range(FC):
                        ins = t_.matmul(ps[:, 0:D], hT[:, w, c * P:(c + 1) * P],
                                        w2T[:, ds(e * (FC * D) + c * D, D)], start=(c == 0), stop=(c == FC - 1))
                    ins.then_inc(f_y, 1)

            tiles(pe, body)


_INS = ["x", "adj", "L0_gnn_Wq", "L0_gnn_Wk", "L0_gnn_Wv", "L0_gnn_Wo", "L0_gnn_bo", "L0_ffn_Wg", "L0_ffn_bg",
        "L0_ffn_W1", "L0_ffn_b1", "L0_ffn_W2", "L0_ffn_b2"]


def kernel(**inputs):
    import numpy as _np
    import concourse.bacc as _bacc
    from concourse import mybir as _mybir
    from concourse.bass_utils import run_bass_kernel_spmd as _run

    nc = _bacc.Bacc("TRN2", target_bir_lowering=False, num_devices=1)
    arrays, args = {}, []
    for name in _INS:
        a = _np.ascontiguousarray(inputs[name])
        arrays[f"in_{name}"] = a
        args.append(nc.dram_tensor(f"in_{name}", a.shape, _mybir.dt.from_np(a.dtype), kind="ExternalInput").ap())
    x = arrays["in_x"]
    out = nc.dram_tensor("out_0", x.shape, _mybir.dt.from_np(x.dtype), kind="ExternalOutput").ap()
    adj_moe_kernel(nc, *args, out)
    r = _run(nc, [arrays], core_ids=[0])
    return r.results[0]["out_0"]
```
